# Optimizing a Trainium2 kernel written in Bass

```python
import numpy as np
import jax
import jax.numpy as jnp

def _softmax(x, axis=-1):
    return jax.nn.softmax(x, axis=axis)

def _gelu(x):
    return jax.nn.gelu(x, approximate=True)

def _silu(x):
    return jax.nn.silu(x)

def _sigmoid(x):
    return jax.nn.sigmoid(x)

def _layernorm(x, axis=-1, eps=1e-05):
    m = jnp.mean(x, axis=axis, keepdims=True)
    v = jnp.var(x, axis=axis, keepdims=True)
    return (x - m) / jnp.sqrt(v + eps)

def _scatter_add(tgt, idx, src, axis=0):
    return tgt.at[idx].add(src)

def _segment_sum(src, seg, n):
    return jax.ops.segment_sum(src, seg, n)
kernel_name = 'mk_conv_attn_hybrid_d2_conv_nchw256_r2_681f8a'

def setup_inputs(seed: int=0):
    np.random.seed(seed)
    _w = jnp.asarray

    def _rec_inputs():
        import jax
        import jax.numpy as jnp
        _gk = jax.random.key(seed)
        x = -0.0003929 + 0.9999 * jax.random.normal(jax.random.fold_in(_gk, 1), (16, 128, 32, 32), jnp.float32)
        return x
    x = _rec_inputs()

    def _L0_conv_setup():
        import jax, jax.numpy as jnp
        import numpy as np
        NUM_HEADS = 8
        KEY_DIM = 32
        HEAD_DIM = KEY_DIM // NUM_HEADS
        BN_EPS = 1e-05

        def _dw_conv(x, w, stride):
            return jax.lax.conv_general_dilated(x, w, window_strides=(stride, stride), padding=((1, 1), (1, 1)), dimension_numbers=('NCHW', 'OIHW', 'NCHW'), feature_group_count=x.shape[1])

        def _bn(x, gamma, beta, mean, var):
            scale = (gamma / jnp.sqrt(var + BN_EPS))[None, :, None, None]
            return (x - mean[None, :, None, None]) * scale + beta[None, :, None, None]
        key = jax.random.key(seed)
        ks = jax.random.split(key, 16)
        C = 128
        inp = {'x': jax.random.normal(ks[0], (16, C, 32, 32), dtype=jnp.float32), 'qW': jax.random.normal(ks[1], (NUM_HEADS * KEY_DIM, C), dtype=jnp.float32) * 0.02, 'kW': jax.random.normal(ks[2], (KEY_DIM, C), dtype=jnp.float32) * 0.02, 'vW': jax.random.normal(ks[3], (KEY_DIM, C), dtype=jnp.float32) * 0.02, 'oW': jax.random.normal(ks[4], (C, NUM_HEADS * KEY_DIM), dtype=jnp.float32) * 0.02, 'kdwW': jax.random.normal(ks[5], (C, 1, 3, 3), dtype=jnp.float32) * 0.1, 'kdw_gamma': jax.random.uniform(ks[6], (C,), minval=0.5, maxval=1.5), 'kdw_beta': jax.random.normal(ks[7], (C,)) * 0.1, 'kdw_mean': jax.random.normal(ks[8], (C,)) * 0.1, 'kdw_var': jax.random.uniform(ks[9], (C,), minval=0.5, maxval=1.5), 'vdwW': jax.random.normal(ks[10], (C, 1, 3, 3), dtype=jnp.float32) * 0.1, 'vdw_gamma': jax.random.uniform(ks[11], (C,), minval=0.5, maxval=1.5), 'vdw_beta': jax.random.normal(ks[12], (C,)) * 0.1, 'vdw_mean': jax.random.normal(ks[13], (C,)) * 0.1, 'vdw_var': jax.random.uniform(ks[14], (C,), minval=0.5, maxval=1.5)}
        return inp
    _L0_conv_all = _L0_conv_setup()
    _L0_conv_in = {k: v for k, v in _L0_conv_all.items() if k in ('qW', 'kW', 'vW', 'oW', 'kdwW', 'kdw_gamma', 'kdw_beta', 'kdw_mean', 'kdw_var', 'vdwW', 'vdw_gamma', 'vdw_beta', 'vdw_mean', 'vdw_var')}
    del _L0_conv_all

    def _L1_attn_setup():
        import jax, jax.numpy as jnp
        import numpy as np
        EPS = 1e-09
        key = jax.random.key(seed)
        kE, kQ, kK, kV = jax.random.split(key, 4)
        B, S, D = (8, 1024, 128)
        return {'E': jax.random.normal(kE, (B, S, D), dtype=jnp.float32), 'WQ': jax.random.normal(kQ, (D, D), dtype=jnp.float32) * (1.0 / np.sqrt(D)), 'WK': jax.random.normal(kK, (D, D), dtype=jnp.float32) * (1.0 / np.sqrt(D)), 'WV': jax.random.normal(kV, (D, D), dtype=jnp.float32) * (1.0 / np.sqrt(D))}
    _L1_attn_all = _L1_attn_setup()
    _L1_attn_in = {k: v for k, v in _L1_attn_all.items() if k in ('WQ', 'WK', 'WV')}
    del _L1_attn_all

    def _L1_ffn_setup():
        import jax, jax.numpy as jnp
        import numpy as np
        N_EXPERTS = 8
        TOP_K = 2
        key = jax.random.key(seed)
        ks = jax.random.split(key, 5)
        B, T, C, E, H = (8, 1024, 128, 8, 341)
        scale = 1.0 / np.sqrt(C)
        return {'x': jax.random.normal(ks[0], (B, T, C), dtype=jnp.float32), 'router_w': jax.random.normal(ks[1], (E, C), dtype=jnp.float32) * scale, 'w1': jax.random.normal(ks[2], (E, H, C), dtype=jnp.float32) * scale, 'w2': jax.random.normal(ks[3], (E, C, H), dtype=jnp.float32) * (1.0 / np.sqrt(H)), 'w3': jax.random.normal(ks[4], (E, H, C), dtype=jnp.float32) * scale}
    _L1_ffn_all = _L1_ffn_setup()
    _L1_ffn_in = {k: v for k, v in _L1_ffn_all.items() if k in ('router_w', 'w1', 'w2', 'w3')}
    del _L1_ffn_all
    return {'x': x, 'L0_conv_qW': _L0_conv_in['qW'], 'L0_conv_kW': _L0_conv_in['kW'], 'L0_conv_vW': _L0_conv_in['vW'], 'L0_conv_oW': _L0_conv_in['oW'], 'L0_conv_kdwW': _L0_conv_in['kdwW'], 'L0_conv_kdw_gamma': _L0_conv_in['kdw_gamma'], 'L0_conv_kdw_beta': _L0_conv_in['kdw_beta'], 'L0_conv_kdw_mean': _L0_conv_in['kdw_mean'], 'L0_conv_kdw_var': _L0_conv_in['kdw_var'], 'L0_conv_vdwW': _L0_conv_in['vdwW'], 'L0_conv_vdw_gamma': _L0_conv_in['vdw_gamma'], 'L0_conv_vdw_beta': _L0_conv_in['vdw_beta'], 'L0_conv_vdw_mean': _L0_conv_in['vdw_mean'], 'L0_conv_vdw_var': _L0_conv_in['vdw_var'], 'L1_attn_WQ': _L1_attn_in['WQ'], 'L1_attn_WK': _L1_attn_in['WK'], 'L1_attn_WV': _L1_attn_in['WV'], 'L1_ffn_router_w': _L1_ffn_in['router_w'], 'L1_ffn_w1': _L1_ffn_in['w1'], 'L1_ffn_w2': _L1_ffn_in['w2'], 'L1_ffn_w3': _L1_ffn_in['w3']}

def reference(x, L0_conv_qW, L0_conv_kW, L0_conv_vW, L0_conv_oW, L0_conv_kdwW, L0_conv_kdw_gamma, L0_conv_kdw_beta, L0_conv_kdw_mean, L0_conv_kdw_var, L0_conv_vdwW, L0_conv_vdw_gamma, L0_conv_vdw_beta, L0_conv_vdw_mean, L0_conv_vdw_var, L1_attn_WQ, L1_attn_WK, L1_attn_WV, L1_ffn_router_w, L1_ffn_w1, L1_ffn_w2, L1_ffn_w3):
    import jax
    import jax.numpy as jnp

    def _L0_conv_ref(x, qW, kW, vW, oW, kdwW, kdw_gamma, kdw_beta, kdw_mean, kdw_var, vdwW, vdw_gamma, vdw_beta, vdw_mean, vdw_var):
        import jax, jax.numpy as jnp
        import numpy as np
        NUM_HEADS = 8
        KEY_DIM = 32
        HEAD_DIM = KEY_DIM // NUM_HEADS
        BN_EPS = 1e-05

        def _dw_conv(x, w, stride):
            return jax.lax.conv_general_dilated(x, w, window_strides=(stride, stride), padding=((1, 1), (1, 1)), dimension_numbers=('NCHW', 'OIHW', 'NCHW'), feature_group_count=x.shape[1])

        def _bn(x, gamma, beta, mean, var):
            scale = (gamma / jnp.sqrt(var + BN_EPS))[None, :, None, None]
            return (x - mean[None, :, None, None]) * scale + beta[None, :, None, None]
        B, C, H, W = x.shape
        q = jnp.einsum('bchw,oc->bohw', x, qW)
        px = q.shape[2]
        q = q.reshape(B, NUM_HEADS, -1, KEY_DIM)
        k = _bn(_dw_conv(x, kdwW, 2), kdw_gamma, kdw_beta, kdw_mean, kdw_var)
        k = jnp.einsum('bchw,oc->bohw', k, kW)
        v = _bn(_dw_conv(x, vdwW, 2), vdw_gamma, vdw_beta, vdw_mean, vdw_var)
        v = jnp.einsum('bchw,oc->bohw', v, vW)
        k = k.reshape(B, KEY_DIM, -1)
        v = v.reshape(B, -1, KEY_DIM)
        attn = jnp.einsum('bnqd,bdl->bnql', q, k) / HEAD_DIM ** 0.5
        attn = jax.nn.softmax(attn, axis=-1)
        ctx = jnp.einsum('bnql,bld->bnqd', attn, v)
        ctx = ctx.reshape(B, NUM_HEADS * KEY_DIM, px, px)
        out = jnp.einsum('bchw,oc->bohw', ctx, oW)
        return out

    def _L1_attn_ref(E, WQ, WK, WV):
        import jax, jax.numpy as jnp
        import numpy as np
        EPS = 1e-09
        D = E.shape[-1]
        scale = jnp.asarray(np.sqrt(D), dtype=E.dtype)
        Q = jnp.einsum('bsd,ed->bse', E, WQ)
        K = jnp.einsum('bsd,ed->bse', E, WK)
        V = jnp.einsum('bsd,ed->bse', E, WV)
        W = jnp.einsum('bqd,bkd->bqk', Q, K) / scale
        S_len = W.shape[-1]
        tril = jnp.tril(jnp.ones((S_len, S_len), dtype=W.dtype))
        M = jnp.where(W == 0, jnp.zeros_like(W), tril[None, :, :])
        x_max = jnp.max(W, axis=-1, keepdims=True)
        x_exp = jnp.exp(W - x_max) * M
        A = x_exp / (jnp.sum(x_exp, axis=-1, keepdims=True) + EPS)
        return jnp.einsum('bqk,bkd->bqd', A, V)

    def _L1_ffn_ref(x, router_w, w1, w2, w3):
        import jax, jax.numpy as jnp
        import numpy as np
        N_EXPERTS = 8
        TOP_K = 2
        B, T, C = x.shape
        flat = x.reshape(-1, C)
        logits = flat @ router_w.T
        probs = jax.nn.softmax(logits, axis=-1)
        topk_probs, topk_idx = jax.lax.top_k(probs, TOP_K)
        topk_probs = topk_probs / (jnp.sum(topk_probs, axis=-1, keepdims=True) + 1e-09)
        onehot = jax.nn.one_hot(topk_idx, N_EXPERTS, dtype=flat.dtype)
        gates = jnp.einsum('nk,nke->ne', topk_probs, onehot)
        h1 = jnp.einsum('nc,ehc->neh', flat, w1)
        h3 = jnp.einsum('nc,ehc->neh', flat, w3)
        h = jax.nn.silu(h1) * h3
        y = jnp.einsum('neh,ech->nec', h, w2)
        out = jnp.einsum('ne,nec->nc', gates, y)
        return out.reshape(B, T, C)

    def _gn(v, G=32, eps=1e-05):
        B_, C_, H_, W_ = v.shape
        g = v.reshape(B_, G, C_ // G, H_, W_)
        m = jnp.mean(g, axis=(2, 3, 4), keepdims=True)
        s = jnp.var(g, axis=(2, 3, 4), keepdims=True)
        return ((g - m) / jnp.sqrt(s + eps)).reshape(v.shape)

    def _ln_c(v, eps=1e-06):
        m = jnp.mean(v, axis=1, keepdims=True)
        s = jnp.var(v, axis=1, keepdims=True)
        return (v - m) / jnp.sqrt(s + eps)

    def _ln_t(v, eps=1e-05):
        m = jnp.mean(v, axis=-1, keepdims=True)
        s = jnp.var(v, axis=-1, keepdims=True)
        return (v - m) / jnp.sqrt(s + eps)

    def _to_tokens(v):
        B_, C_, H_, W_ = v.shape
        return v.reshape(B_, C_, H_ * W_).transpose(0, 2, 1)

    def _from_tokens(t, like):
        B_, C_, H_, W_ = like.shape
        return t.transpose(0, 2, 1).reshape(B_, C_, H_, W_)
    x = x + _L0_conv_ref(_gn(x), L0_conv_qW, L0_conv_kW, L0_conv_vW, L0_conv_oW, L0_conv_kdwW, L0_conv_kdw_gamma, L0_conv_kdw_beta, L0_conv_kdw_mean, L0_conv_kdw_var, L0_conv_vdwW, L0_conv_vdw_gamma, L0_conv_vdw_beta, L0_conv_vdw_mean, L0_conv_vdw_var)
    t = _to_tokens(x)
    t = t + _L1_attn_ref(_ln_t(t), L1_attn_WQ, L1_attn_WK, L1_attn_WV)
    t = t + _L1_ffn_ref(_ln_t(t), L1_ffn_router_w, L1_ffn_w1, L1_ffn_w2, L1_ffn_w3)
    x = _from_tokens(t, x)
    return x

_drawn_inputs = setup_inputs


def setup_inputs(seed=0):
    import zlib

    import numpy as np

    out = dict(_drawn_inputs(seed))
    spreads = {}
    factors = {'L0_conv_qW': 8.0,
     'L0_conv_kW': 8.0,
     'L0_conv_vW': 7.502,
     'L0_conv_oW': 6.249,
     'L0_conv_kdwW': 8.0,
     'L0_conv_kdw_gamma': 8.0,
     'L0_conv_kdw_beta': 64.0,
     'L0_conv_kdw_mean': 64.0,
     'L0_conv_kdw_var': 8.0,
     'L0_conv_vdwW': 8.0,
     'L0_conv_vdw_gamma': 8.0,
     'L0_conv_vdw_beta': 8.0,
     'L0_conv_vdw_mean': 7.183,
     'L0_conv_vdw_var': 8.0,
     'L1_attn_WQ': 8.0,
     'L1_attn_WK': 8.0,
     'L1_attn_WV': 7.115,
     'L1_ffn_router_w': 3.772,
     'L1_ffn_w1': 3.611,
     'L1_ffn_w2': 3.416,
     'L1_ffn_w3': 3.409}
    for name, (base, spread) in spreads.items():
        noise = np.random.default_rng([zlib.crc32(name.encode()), seed]).standard_normal(out[name].shape)
        drawn = base * np.exp(spread * noise) if base else spread * noise
        out[name] = jnp.asarray(drawn.astype(out[name].dtype))
    for name, factor in factors.items():
        out[name] = (out[name] * factor).astype(out[name].dtype)
    return out
```

```python
from contextlib import ExitStack

import concourse.bass as bass
from concourse import mybir

ALU = mybir.AluOpType
ACT = mybir.ActivationFunctionType
AX_X = mybir.AxisListType.X
F32 = mybir.dt.float32
F32R = mybir.dt.float32r

P = 128
HW = 1024
SIDE = 32
CP = 256
CT = CP // P
KD = 32
L = 256
LT = L // P
ROWS = SIDE
PAIRS = ROWS // 2
TAPS = 9
GN_GROUP = 4
GN_EPS = 1e-5
BN_EPS = 1e-5
COPIES = 3
STACK = COPIES * KD
TURN = 66
Q_CHUNKS = 4
FRONT_USES = 3 + Q_CHUNKS
Q_STEPS = (6, 9, 12, 15)
OUT_USES = 2


def wait(eng, sem, value):
    if isinstance(value, int) and value <= 0:
        return
    eng.wait_ge(sem, value)


def over_images(eng, n, period):
    period(0)
    if n > 2:
        with eng.Fori(1, n - 1) as b:
            period(b)
    period(n - 1)


def conv_attention(nc, X, ident, dram):
    NB = X.shape[1]
    with ExitStack() as ctx:
        def sb(name, shape, dt=F32):
            return ctx.enter_context(nc.sbuf_tensor(name, shape, dt))

        def ps(name, shape):
            return ctx.enter_context(nc.psum_tensor(name, shape, F32))

        def sem(name):
            return ctx.enter_context(nc.semaphore(name))

        group_mean = sb("group_mean", [P, P])
        minus_half = sb("minus_half", [P, 2])
        qwT = sb("qwT", [P, CP])
        kwT = sb("kwT", [P, KD])
        vwT = sb("vwT", [P, KD])
        owT = sb("owT", [P, CT, P])
        kdw = sb("kdw", [P, TAPS])
        vdw = sb("vdw", [P, TAPS])
        bn = sb("bn", [P, 4, 2])
        bn_ve = sb("bn_ve", [P, 2])
        bn_rs = sb("bn_rs", [P, 2])
        bn_scale = sb("bn_scale", [P, 2])
        bn_ms = sb("bn_ms", [P, 2])
        bn_shift = sb("bn_shift", [P, 2])
        tap_scale = sb("tap_scale", [P, 2, TAPS])
        kv_w = sb("kv_w", [P, P])
        tap_w = sb("tap_w", [P, TAPS, P])
        kv_bias = sb("kv_bias", [P, 1])
        xn = sb("xn", [P, SIDE, SIDE])
        bn_st = sb("bn_st", [P, 2, 6])
        mv = sb("mv", [P, 2])
        dmean = sb("dmean", [P, 1])
        gmean = sb("gmean", [P, 1])
        spread = sb("spread", [P, 1])
        gvar = sb("gvar", [P, 1])
        grs = sb("grs", [P, 1])
        kv = sb("kv", [P, L])
        k_high = sb("k_high", [P, L], F32R)
        k_stack = sb("k_stack", [STACK, L], F32R)
        v_flat = sb("v_flat", [P, L])
        v_ones = sb("v_ones", [P, LT, KD + 1])
        q_high = sb("q_high", [P, ROWS // 4, CP], F32R)
        q_low = sb("q_low", [P, ROWS // 4, CP], F32R)
        q_stack = sb("q_stack", [STACK, ROWS, CP], F32R)
        neg_max = sb("neg_max", [P, ROWS, CT])
        probs = sb("probs", [P, 2, CT, L])
        probsT = sb("probsT", [P, 2, LT, 2, CP])
        ctxT = sb("ctxT", [TURN, 2, 2 * CP])
        rsum = sb("rsum", [P, 2, 4])
        context = sb("context", [P, CT, ROWS, KD])

        s_bank = [ps(f"s_bank{i}", [P, CT, L]) for i in range(2)]
        t_bank = [ps(f"t_bank{i}", [P, LT, CP]) for i in range(2)]
        o_bank = ps("o_bank", [P, 2 * CP])
        c_bank = ps("c_bank", [P, 4, TURN])
        front = ps("front", [P, 512])

        weights_in = sem("weights_in")
        first_in = sem("first_in")
        rest_in = sem("rest_in")
        consts = sem("consts")
        bn_eps_added = sem("bn_eps_added")
        bn_rsqrt = sem("bn_rsqrt")
        setup_step = sem("setup_step")
        weights_ready = sem("weights_ready")
        bias_mm = sem("bias_mm")
        bias_ready = sem("bias_ready")
        chan_stats_ready = sem("chan_stats_ready")
        gmean_ready = sem("gmean_ready")
        dmean_ready = sem("dmean_ready")
        spread_ready = sem("spread_ready")
        k_high_ready = sem("k_high_ready")
        rsum_ready = sem("rsum_ready")
        gvar_ready = sem("gvar_ready")
        grs_ready = sem("grs_ready")
        xn_ready = sem("xn_ready")
        front_full = sem("front_full")
        kv_ready = sem("kv_ready")
        k_ready = sem("k_ready")
        v_staged = sem("v_staged")
        v_in = sem("v_in")
        q_high_done = sem("q_high_done")
        q_low_done = sem("q_low_done")
        q_in = [sem(f"q_in{k}") for k in range(Q_CHUNKS)]
        s_full = sem("s_full")
        max_ready = sem("max_ready")
        probs_full = sem("probs_full")
        t_full = sem("t_full")
        evac_even = sem("evac_even")
        evac_odd = sem("evac_odd")
        o_full = sem("o_full")
        ctxT_full = sem("ctxT_full")
        c_full = sem("c_full")
        ctx_done = sem("ctx_done")
        out_done = sem("out_done")

        N_WEIGHTS = 7
        Q_IN = 16 * COPIES * 4
        USES = FRONT_USES + OUT_USES

        def front_count(b, k):
            if isinstance(b, int) and b == 0:
                return k
            return FRONT_USES + (b - 1) * USES + k + (k == FRONT_USES - 1)

        def out_count(b, k):
            if isinstance(b, int) and b == NB - 1:
                return FRONT_USES + b * USES + k
            return FRONT_USES + b * USES + FRONT_USES - 1 + 2 * k

        def has_next(b):
            return not (isinstance(b, int) and b == NB - 1)

        with nc.Block() as block:

            @block.sync
            def _(sp):
                sp.dma_start(X[:, 0, :], dram["x"][0]).then_inc(first_in, 16)
                for tile, src in ((qwT, dram["qWT"]), (kwT, dram["kWT"]), (vwT, dram["vWT"]),
                                  (kdw, dram["kdw"]), (vdw, dram["vdw"])):
                    sp.dma_start(tile[:], src).then_inc(weights_in, 16)
                sp.dma_start(owT[:], dram["oWT"].rearrange("(t p) o -> p t o", p=P)).then_inc(weights_in, 16)
                sp.dma_start(bn[:], dram["bn"]).then_inc(weights_in, 16)
                sp.dma_start(X[:, 1:, :], dram["x"][1:].rearrange("b p n -> p b n")).then_inc(rest_in, 16)

                def stack(b):
                    for k in range(Q_CHUNKS):
                        sp.wait_ge(q_low_done, Q_CHUNKS * b + k + 1)
                        for r, part in enumerate((q_high, q_low, q_high)):
                            for j in range(4):
                                sp.dma_start(q_stack[r * KD:(r + 1) * KD, 8 * k + j:8 * (k + 1):4, :].bitcast(F32),
                                             part[j * KD:(j + 1) * KD, 2 * k:2 * k + 2, :].bitcast(F32)
                                             ).then_inc(q_in[k], 16)
                    sp.wait_ge(v_staged, b + 1)
                    for t in range(LT):
                        sp.dma_start(v_ones[:, t, 0:KD],
                                     v_flat[STACK + 16 * t:STACK + 16 * (t + 1), :]).then_inc(v_in, 16)

                stack(0)
                if NB > 1:
                    with sp.Fori(1, NB) as b:
                        stack(b)

            @block.gpsimd
            def _(pool):
                pool.memset(minus_half[:], -0.5).then_inc(consts, 1)
                pool.memset(ident[:], 0.0).then_inc(consts, 1)
                pool.memset(group_mean[:], 1.0 / GN_GROUP).then_inc(consts, 1)
                pool.wait_ge(consts, 3)
                pool.affine_select(out=ident[:], in_=ident[:], compare_op=ALU.not_equal, fill=1.0, base=0,
                                   pattern=[[-1, P]], channel_multiplier=1).then_inc(consts, 1)
                blocks = group_mean[:].rearrange("p (g i) -> p g i", i=GN_GROUP)
                pool.affine_select(out=blocks, in_=blocks, compare_op=ALU.is_ge, fill=0.0, base=0,
                                   pattern=[[-GN_GROUP, P // GN_GROUP], [0, GN_GROUP]],
                                   channel_multiplier=1).then_inc(consts, 1)
                pool.wait_ge(consts, 5)
                pool.affine_select(out=blocks, in_=blocks, compare_op=ALU.is_ge, fill=0.0, base=GN_GROUP - 1,
                                   pattern=[[GN_GROUP, P // GN_GROUP], [0, GN_GROUP]],
                                   channel_multiplier=-1).then_inc(consts, 1)
                pool.wait_ge(bn_eps_added, 1)
                pool.tensor_tensor(bn_rs[:], bn_ve[:], minus_half[:], ALU.pow).then_inc(bn_rsqrt, 1)
                with pool.Fori(0, NB) as b:
                    pool.wait_ge(gvar_ready, b + 1)
                    pool.tensor_tensor(grs[:], gvar[:], minus_half[:, 0:1], ALU.pow).then_inc(grs_ready, 1)

            @block.vector
            def _(dve):
                steps = [0]

                def link(ins):
                    ins.then_inc(setup_step, 1)
                    steps[0] += 1
                    dve.wait_ge(setup_step, steps[0])

                dve.memset(v_ones[:, :, KD:KD + 1], 1.0)
                dve.memset(ctxT[:], 0.0).then_inc(weights_ready, 1)
                dve.wait_ge(weights_in, 16 * N_WEIGHTS)
                gamma, beta, mean, var = (bn[:, i, :] for i in range(4))
                dve.tensor_scalar(bn_ve[:], var, BN_EPS, None, ALU.add).then_inc(bn_eps_added, 1)
                for r in range(COPIES):
                    link(dve.tensor_scalar(kv_w[:, r * KD:(r + 1) * KD], kwT[:], 0.5, None, ALU.mult))
                link(dve.tensor_copy(kv_w[:, STACK:], vwT[:]))
                dve.wait_ge(bn_rsqrt, 1)
                link(dve.tensor_tensor(bn_scale[:], gamma, bn_rs[:], ALU.mult))
                link(dve.tensor_tensor(bn_ms[:], mean, bn_scale[:], ALU.mult))
                link(dve.tensor_tensor(bn_shift[:], beta, bn_ms[:], ALU.subtract))
                link(dve.tensor_scalar(tap_scale[:, 0, :], kdw[:], bn_scale[:, 0:1], None, ALU.mult))
                link(dve.tensor_scalar(tap_scale[:, 1, :], vdw[:], bn_scale[:, 1:2], None, ALU.mult))
                for t in range(TAPS):
                    dve.tensor_scalar(tap_w[:, t, 0:STACK], kv_w[:, 0:STACK], tap_scale[:, 0, t:t + 1], None, ALU.mult)
                    last = dve.tensor_scalar(tap_w[:, t, STACK:], kv_w[:, STACK:], tap_scale[:, 1, t:t + 1], None,
                                             ALU.mult)
                last.then_inc(weights_ready, 1)
                dve.wait_ge(bias_mm, 1)
                dve.tensor_copy(kv_bias[0:STACK, :], front[0:STACK, 0:1]).then_inc(bias_ready, 1)
                dve.tensor_copy(kv_bias[STACK:, :], front[STACK:, 1:2]).then_inc(bias_ready, 1)
                dve.wait_ge(bias_ready, 2)

                def channel_stats(b):
                    for i in range(2):
                        dve.bn_stats(bn_st[:, i, :], X[:, b, 512 * i:512 * (i + 1)])
                    dve.drain()
                    dve.bn_aggr(mv[:], bn_st[:]).then_inc(chan_stats_ready, 1)

                def group_spread(b):
                    dve.wait_ge(front_full, front_count(b, 0) + 1)
                    dve.tensor_copy(gmean[:], front[:, 0:1]).then_inc(gmean_ready, 1)
                    dve.wait_ge(gmean_ready, b + 1)
                    dve.tensor_tensor(dmean[:], mv[:, 0:1], gmean[:], ALU.subtract).then_inc(dmean_ready, 1)
                    dve.wait_ge(dmean_ready, b + 1)
                    dve.scalar_tensor_tensor(out=spread[:], in0=dmean[:], scalar=dmean[:], in1=mv[:, 1:2],
                                             op0=ALU.mult, op1=ALU.add).then_inc(spread_ready, 1)

                def group_variance(b):
                    dve.wait_ge(front_full, front_count(b, 1) + 1)
                    dve.tensor_scalar(gvar[:], front[:, 1:2], GN_EPS, None, ALU.add).then_inc(gvar_ready, 1)

                def group_norm(b):
                    dve.wait_ge(grs_ready, b + 1)
                    dve.tensor_scalar(xn[:].rearrange("p h w -> p (h w)"), X[:, b, :], gmean[:], grs[:],
                                      ALU.subtract, ALU.mult).then_inc(xn_ready, 1)

                def keys_values(b):
                    dve.wait_ge(front_full, front_count(b, 2) + 1)
                    dve.tensor_scalar(kv[:], front[:, 0:L], kv_bias[:], None, ALU.add).then_inc(kv_ready, 1)

                def split_keys(b):
                    dve.wait_ge(kv_ready, b + 1)
                    wait(dve, s_full, b * ROWS)
                    dve.tensor_copy(k_stack[0:2 * KD, :], kv[0:2 * KD, :])
                    dve.tensor_copy(k_high[2 * KD:STACK, :], kv[2 * KD:STACK, :]).then_inc(k_high_ready, 1)
                    dve.wait_ge(k_high_ready, b + 1)
                    dve.tensor_tensor(k_stack[2 * KD:STACK, :], kv[2 * KD:STACK, :],
                                      k_high[2 * KD:STACK, :].bitcast(F32), ALU.subtract).then_inc(k_ready, 1)

                def stage_values(b):
                    wait(dve, v_in, b * 16 * LT)
                    dve.tensor_copy(v_flat[STACK:, :], kv[STACK:, :]).then_inc(v_staged, 1)

                def query_low(b, k):
                    dve.wait_ge(q_high_done, Q_CHUNKS * b + k + 1)
                    wait(dve, q_in[k], b * Q_IN)
                    dve.tensor_tensor(q_low[:, 2 * k:2 * k + 2, :],
                                      front[:].rearrange("p (g c) -> p g c", c=CP),
                                      q_high[:, 2 * k:2 * k + 2, :].bitcast(F32),
                                      ALU.subtract).then_inc(q_low_done, 1)

                def row_max(b, h):
                    dve.wait_ge(s_full, b * ROWS + h + 1)
                    dve.tensor_reduce(neg_max[:, h, :], s_bank[h % 2][:], AX_X, ALU.max,
                                      negate=True).then_inc(max_ready, 1)

                def evacuate_even(b, p):
                    dve.wait_ge(t_full, b * ROWS + 2 * p + 1)
                    wait(dve, o_full, b * PAIRS + p - 1)
                    dve.tensor_copy(probsT[:, p % 2, :, 0, :], t_bank[0][:]).then_inc(evac_even, 1)

                def normalise(b, p):
                    if p == 0:
                        wait(dve, out_done, OUT_USES * b)
                    dve.wait_ge(c_full, b * PAIRS + p + 1)
                    dve.reciprocal(rsum[:, p % 2, :], c_bank[:, :, KD]).then_inc(rsum_ready, 1)
                    dve.wait_ge(rsum_ready, b * PAIRS + p + 1)
                    dve.tensor_tensor(context[:, :, 2 * p:2 * p + 2, :].rearrange("p t h d -> p h t d"),
                                      c_bank[:, :, 0:KD].rearrange("p (h t) d -> p h t d", t=CT),
                                      rsum[:, p % 2, :].rearrange("p (h t) -> p h t", t=CT).unsqueeze(3)
                                      .to_broadcast([P, 2, CT, KD]), ALU.mult).then_inc(ctx_done, 1)

                def add_output(b, k):
                    dve.wait_ge(front_full, out_count(b, k) + 1)
                    half = X[:, b, 512 * k:512 * (k + 1)]
                    dve.tensor_tensor(half, half, front[:], ALU.add).then_inc(out_done, 1)

                dve.wait_ge(first_in, 16)
                channel_stats(0)
                group_spread(0)
                group_variance(0)
                group_norm(0)
                keys_values(0)
                split_keys(0)
                stage_values(0)
                for k in range(Q_CHUNKS):
                    query_low(0, k)
                if NB > 1:
                    dve.wait_ge(rest_in, 16)

                def period(b):
                    nxt = has_next(b)
                    for i in range(PAIRS + 3):
                        if i < PAIRS:
                            row_max(b, 2 * i)
                            row_max(b, 2 * i + 1)
                        if 1 <= i <= PAIRS:
                            evacuate_even(b, i - 1)
                        if i >= 3:
                            normalise(b, i - 3)
                        if nxt:
                            if i == 0:
                                channel_stats(b + 1)
                            if i == 1:
                                group_spread(b + 1)
                            if i == 2:
                                group_variance(b + 1)
                            if i == 3:
                                group_norm(b + 1)
                            if i == 4:
                                keys_values(b + 1)
                            if i in Q_STEPS:
                                query_low(b + 1, Q_STEPS.index(i))
                            if i == PAIRS + 1:
                                split_keys(b + 1)
                        if i == 13:
                            add_output(b, 0)
                    if nxt:
                        stage_values(b + 1)
                    add_output(b, 1)

                over_images(dve, NB, period)

            @block.scalar
            def _(act):
                def query_high(b, k):
                    act.wait_ge(front_full, front_count(b, 3 + k) + 1)
                    wait(act, q_in[k], b * Q_IN)
                    act.activation(q_high[:, 2 * k:2 * k + 2, :], front[:].rearrange("p (g c) -> p g c", c=CP),
                                   ACT.Copy).then_inc(q_high_done, 1)

                def exps(b, h):
                    act.wait_ge(max_ready, b * ROWS + h + 1)
                    wait(act, t_full, b * ROWS + h - 1)
                    for t in range(CT):
                        last = act.activation(probs[:, h % 2, t, :], s_bank[h % 2][:, t, :], ACT.Exp,
                                              bias=neg_max[:, h, t:t + 1])
                    last.then_inc(probs_full, 1)

                def evacuate_odd(b, p):
                    act.wait_ge(t_full, b * ROWS + 2 * p + 2)
                    wait(act, o_full, b * PAIRS + p - 1)
                    act.activation(probsT[:, p % 2, :, 1, :], t_bank[1][:], ACT.Copy).then_inc(evac_odd, 1)

                def evacuate_context(b, p):
                    act.wait_ge(o_full, b * PAIRS + p + 1)
                    wait(act, c_full, b * PAIRS + p - 1)
                    act.activation(ctxT[0:KD + 1, p % 2, :], o_bank[0:KD + 1, :], ACT.Copy).then_inc(ctxT_full, 1)

                for k in range(Q_CHUNKS):
                    query_high(0, k)
                act.wait_ge(weights_ready, 2)

                def period(b):
                    for i in range(PAIRS + 2):
                        if i < PAIRS:
                            exps(b, 2 * i)
                            exps(b, 2 * i + 1)
                        if 1 <= i <= PAIRS:
                            evacuate_odd(b, i - 1)
                        if i >= 2:
                            evacuate_context(b, i - 2)
                        if has_next(b) and i in Q_STEPS:
                            query_high(b + 1, Q_STEPS.index(i))

                over_images(act, NB, period)

            @block.tensor
            def _(pe):
                pe.wait_ge(weights_in, 16 * N_WEIGHTS)
                pe.wait_ge(weights_ready, 2)
                pe.wait_ge(consts, 6)
                pe.matmul(front[:, 0:2], kv_w[:], bn_shift[:], start=True, stop=True).then_inc(bias_mm, 1)
                pe.wait_ge(bias_ready, 2)

                def group_sum(b, k, ready, column):
                    pe.wait_ge(ready, b + 1)
                    pe.matmul(front[:, k:k + 1], group_mean[:], column, start=True, stop=True).then_inc(front_full, 1)

                def keys_values(b):
                    pe.wait_ge(xn_ready, b + 1)
                    pe.wait_ge(gvar_ready, b + 1)
                    out = front[:, 0:L].rearrange("p (i j) -> p i j", j=SIDE // 2)
                    for n, t in enumerate((4, 0, 1, 2, 3, 5, 6, 7, 8)):
                        di, dj = divmod(t, 3)
                        last = pe.matmul(out[:, di == 0:, dj == 0:], tap_w[:, t, :],
                                         xn[:, (1, 0, 1)[di]:SIDE - (di == 0):2, (1, 0, 1)[dj]:SIDE - (dj == 0):2],
                                         start=(n == 0), stop=(n == TAPS - 1), skip_group_check=True)
                    last.then_inc(front_full, 1)

                def queries(b, k):
                    if k == 0:
                        pe.wait_ge(kv_ready, b + 1)
                    elif k < Q_CHUNKS - 1:
                        pe.wait_ge(q_low_done, Q_CHUNKS * b + k)
                    else:
                        pe.wait_ge(q_low_done, Q_CHUNKS * b + k)
                        wait(pe, out_done, OUT_USES * (b - 1) + 1)
                    for i in range(2):
                        g = 2 * k + i
                        last = pe.matmul(front[:, i * CP:(i + 1) * CP], xn[:, 4 * g:4 * (g + 1), :].rearrange("p h w -> p (h w)"), qwT[:],
                                         start=(i == 0), stop=(i == 1), skip_group_check=True)
                    last.then_inc(front_full, 1)

                def scores(b, h):
                    if h == 0:
                        pe.wait_ge(k_ready, b + 1)
                    if h % 8 == 0:
                        pe.wait_ge(q_in[h // 8], (b + 1) * Q_IN)
                    wait(pe, probs_full, b * ROWS + h - 1)
                    for t in range(CT):
                        last = pe.matmul(s_bank[h % 2][:, t, :], q_stack[:, h, t * P:(t + 1) * P], k_stack[:],
                                         start=(t == 0), stop=(t == CT - 1), skip_group_check=True)
                    last.then_inc(s_full, 1)

                def transposes(b, h):
                    pe.wait_ge(probs_full, b * ROWS + h + 1)
                    wait(pe, (evac_even, evac_odd)[h % 2], b * PAIRS + h // 2)
                    for lt in range(LT):
                        for t in range(CT):
                            last = pe.transpose(t_bank[h % 2][:, lt, t * P:(t + 1) * P],
                                                probs[:, h % 2, t, lt * P:(lt + 1) * P], ident[:])
                    last.then_inc(t_full, 1)

                def values(b, p):
                    if p == 0:
                        pe.wait_ge(v_in, (b + 1) * 16 * LT)
                    pe.wait_ge(evac_even, b * PAIRS + p + 1)
                    pe.wait_ge(evac_odd, b * PAIRS + p + 1)
                    wait(pe, ctxT_full, b * PAIRS + p)
                    for lt in range(LT):
                        last = pe.matmul(o_bank[0:KD + 1, :], v_ones[:, lt, :],
                                         probsT[:, p % 2, lt, :, :], start=(lt == 0), stop=(lt == LT - 1))
                    last.then_inc(o_full, 1)

                def turn_context(b, p):
                    pe.wait_ge(ctxT_full, b * PAIRS + p + 1)
                    wait(pe, ctx_done, b * PAIRS + p)
                    for n in range(4):
                        last = pe.transpose(c_bank[:, n, :], ctxT[:, p % 2, n * P:(n + 1) * P], ident[0:TURN, 0:TURN])
                    last.then_inc(c_full, 1)

                def project(b, k):
                    pe.wait_ge(ctx_done, b * PAIRS + (k + 1) * PAIRS // 2)
                    if has_next(b):
                        pe.wait_ge(q_low_done, Q_CHUNKS * (b + 1) + Q_CHUNKS - 1 + k)
                    else:
                        pe.wait_ge(out_done, OUT_USES * b + k)
                    for t in range(CT):
                        last = pe.matmul(front[:], owT[:, t, :], context[:, t, 16 * k:16 * (k + 1), :],
                                         start=(t == 0), stop=(t == CT - 1))
                    last.then_inc(front_full, 1)

                def front_part(b, i):
                    if i == 1:
                        wait(pe, out_done, OUT_USES * (b - 1))
                        group_sum(b, 0, chan_stats_ready, mv[:, 0:1])
                    if i == 2:
                        group_sum(b, 1, spread_ready, spread[:])
                    if i == 4:
                        keys_values(b)
                    if i in Q_STEPS:
                        queries(b, Q_STEPS.index(i))

                for i in range(PAIRS):
                    front_part(0, i)

                def period(b):
                    for i in range(PAIRS + 3):
                        if i < PAIRS:
                            scores(b, 2 * i)
                            scores(b, 2 * i + 1)
                        if 1 <= i <= PAIRS:
                            transposes(b, 2 * i - 2)
                            transposes(b, 2 * i - 1)
                        if 2 <= i <= PAIRS + 1:
                            values(b, i - 2)
                        if i >= 3:
                            turn_context(b, i - 3)
                        if has_next(b):
                            front_part(b + 1, i)
                        if i == 13:
                            project(b, 0)
                    project(b, 1)

                over_images(pe, NB, period)


ATTN_EPS = 1e-9
LN_EPS = 1e-5
TT = HW // P
SHARED_USES = 8


def over_pairs_of_images(eng, n, period):
    assert n % 2 == 0
    period(0, 0)
    if n > 2:
        with eng.Fori(0, n // 2 - 1) as pair:
            period(2 * pair + 1, 1)
            period(2 * pair + 2, 0)
    period(n - 1, 1)


def causal_attention(nc, X, ident, dram):
    NB = X.shape[1]
    XT = X[:].rearrange("p b (t c) -> p b t c", c=P)
    with ExitStack() as ctx:
        def sb(name, shape, dt=F32):
            return ctx.enter_context(nc.sbuf_tensor(name, shape, dt))

        def ps(name, shape):
            return ctx.enter_context(nc.psum_tensor(name, shape, F32))

        def sem(name):
            return ctx.enter_context(nc.semaphore(name))

        minus_half = sb("ln_minus_half", [P, TT])
        tril = sb("tril", [P, P])
        wq = sb("wq", [P, P])
        wk = sb("wk", [P, P])
        wvT = sb("wvT", [P, P])
        wqk = sb("wqk", [P, P])
        ln_st = sb("ln_st", [P, TT, 6])
        ln_mv = sb("ln_mv", [P, TT, 2])
        ln_ve = sb("ln_ve", [P, TT])
        ln_rs = sb("ln_rs", [P, TT])
        staged = sb("staged", [P, TT, P])
        e_tok = sb("e_tok", [P, TT, P])
        eT = sb("eT", [P, 2, HW])
        gT = sb("gT", [P, 2, HW])
        val = sb("val", [P, 2, TT, P])
        neg_max = sb("row_neg_max", [P, 2])
        probs = sb("causal_probs", [P, 2, HW])
        probsT = sb("causal_probsT", [P, 2, TT, P])
        row_sum = sb("row_sum", [P, 2])
        row_eps = sb("row_eps", [P, 2])
        row_inv = sb("row_inv", [P, 2])

        s_bank = [ps(f"score_bank{i}", [P, HW]) for i in range(2)]
        t_bank = ps("turn_bank", [P, TT, P])
        o_bank = ps("sum_bank", [P, P])
        shared = ps("shared_bank", [P, 512])

        weights_in = sem("attn_weights_in")
        staged_in = sem("staged_in")
        attn_consts = sem("attn_consts")
        wqk_mm = sem("wqk_mm")
        wqk_ready = sem("wqk_ready")
        shared_full = sem("shared_full")
        shared_free = sem("shared_free")
        mv_ready = sem("ln_mv_ready")
        ve_ready = sem("ln_ve_ready")
        rs_ready = sem("ln_rs_ready")
        e_ready = sem("e_ready")
        s_full = sem("tile_scored")
        max_ready = sem("row_max_ready")
        exp_done = sem("exp_done")
        diag_done = sem("diagonal_masked")
        masked = sem("tile_masked")
        t_full = sem("tile_turned")
        turned_out = sem("tile_turned_out")
        o_full = sem("tile_summed")
        eps_added = sem("eps_added")
        inv_ready = sem("row_inv_ready")
        added = sem("tile_added")

        def has_next(b):
            return not (isinstance(b, int) and b == NB - 1)

        with nc.Block() as block:

            @block.sync
            def _(sp):
                for tile, src in ((wq, dram["wq"]), (wk, dram["wk"]), (wvT, dram["wvT"])):
                    sp.dma_start(tile[:], src).then_inc(weights_in, 16)

                def stage(b):
                    wait(sp, shared_free, SHARED_USES * (b - 1) + 2)
                    sp.dma_start(staged[:], XT[:, b, :, :]).then_inc(staged_in, 16)

                stage(0)
                with sp.Fori(1, NB) as b:
                    stage(b)

            @block.gpsimd
            def _(pool):
                pool.memset(tril[:], 1.0).then_inc(attn_consts, 1)
                pool.memset(minus_half[:], -0.5).then_inc(attn_consts, 1)
                pool.wait_ge(attn_consts, 2)
                pool.affine_select(out=tril[:], in_=tril[:], compare_op=ALU.is_ge, fill=0.0, base=0,
                                   pattern=[[-1, P]], channel_multiplier=1).then_inc(attn_consts, 1)
                pool.wait_ge(attn_consts, 3)

                def rsqrt(b):
                    pool.wait_ge(ve_ready, b + 1)
                    pool.tensor_tensor(ln_rs[:], ln_ve[:], minus_half[:], ALU.pow).then_inc(rs_ready, 1)

                rsqrt(0)

                def period(b, slot):
                    for i in range(TT):
                        pool.wait_ge(exp_done, b * TT + i + 1)
                        block_ = probs[:, i % 2, i * P:(i + 1) * P]
                        pool.tensor_tensor(block_, block_, tril[:], ALU.mult).then_inc(diag_done, 1)
                        if i == 2 and has_next(b):
                            rsqrt(b + 1)

                over_pairs_of_images(pool, NB, period)

            @block.vector
            def _(dve):
                dve.wait_ge(wqk_mm, 1)
                dve.tensor_scalar(wqk[:], shared[:, 0:P], float(P) ** -0.5, None, ALU.mult).then_inc(wqk_ready, 1)

                def token_stats(b):
                    dve.wait_ge(shared_free, SHARED_USES * b + 2)
                    for t in range(TT):
                        dve.bn_stats(ln_st[:, t, :], XT[:, b, t, :])
                    dve.drain()
                    for t in range(TT):
                        last = dve.bn_aggr(ln_mv[:, t, :], ln_st[:, t, :])
                    last.then_inc(mv_ready, 1)
                    dve.wait_ge(mv_ready, b + 1)
                    dve.tensor_scalar(ln_ve[:], ln_mv[:, :, 1], LN_EPS, None, ALU.add).then_inc(ve_ready, 1)

                def token_norm(b):
                    dve.wait_ge(rs_ready, b + 1)
                    wait(dve, shared_full, SHARED_USES * b + 2)
                    for t in range(TT):
                        last = dve.tensor_scalar(e_tok[:, t, :], XT[:, b, t, :], ln_mv[:, t, 0:1],
                                                 ln_rs[:, t:t + 1], ALU.subtract, ALU.mult)
                    last.then_inc(e_ready, 1)

                def tile_max(b, i):
                    dve.wait_ge(s_full, b * TT + i + 1)
                    wait(dve, exp_done, b * TT + i - 1)
                    dve.tensor_reduce(neg_max[:, i % 2:i % 2 + 1], s_bank[i % 2][:], AX_X, ALU.max,
                                      negate=True).then_inc(max_ready, 1)

                def mask(b, i):
                    n = (i + 1) * P
                    dve.wait_ge(diag_done, b * TT + i + 1)
                    dve.scalar_tensor_tensor(out=probs[:, i % 2, 0:n], in0=s_bank[i % 2][:, 0:n], scalar=0.0,
                                             in1=probs[:, i % 2, 0:n], op0=ALU.not_equal, op1=ALU.mult,
                                             accum_out=row_sum[:, i % 2:i % 2 + 1]).then_inc(masked, 1)
                    dve.wait_ge(masked, b * TT + i + 1)
                    dve.tensor_scalar(row_eps[:, i % 2:i % 2 + 1], row_sum[:, i % 2:i % 2 + 1], ATTN_EPS, None,
                                      ALU.add).then_inc(eps_added, 1)
                    dve.wait_ge(eps_added, b * TT + i + 1)
                    dve.reciprocal(row_inv[:, i % 2:i % 2 + 1], row_eps[:, i % 2:i % 2 + 1]).then_inc(inv_ready, 1)

                def add(b, i):
                    dve.wait_ge(inv_ready, b * TT + i + 1)
                    dve.wait_ge(o_full, b * TT + i + 1)
                    dve.scalar_tensor_tensor(out=XT[:, b, i, :], in0=o_bank[:], scalar=row_inv[:, i % 2:i % 2 + 1],
                                             in1=XT[:, b, i, :], op0=ALU.mult, op1=ALU.add).then_inc(added, 1)

                token_stats(0)
                token_norm(0)

                def period(b, slot):
                    tile_max(b, 0)
                    for i in range(TT + 1):
                        if i + 1 < TT:
                            tile_max(b, i + 1)
                        if i < TT:
                            mask(b, i)
                        if i >= 1:
                            add(b, i - 1)
                        if has_next(b):
                            if i == 2:
                                token_stats(b + 1)
                            if i == 3:
                                token_norm(b + 1)

                over_pairs_of_images(dve, NB, period)

            @block.scalar
            def _(act):
                def shared_out(b, slot, k):
                    h = k % 2
                    half = slice(512 * h, 512 * (h + 1))
                    tiles = slice(TT // 2 * h, TT // 2 * (h + 1))
                    dst = (XT[:, b, tiles, :], eT[:, slot, half], gT[:, slot, half], val[:, slot, tiles, :])[k // 2]
                    act.wait_ge(shared_full, SHARED_USES * b + k + 1)
                    src = shared[:].rearrange("p (t c) -> p t c", c=P) if k // 2 in (0, 3) else shared[:]
                    act.activation(dst, src, ACT.Copy).then_inc(shared_free, 1)

                def exps(b, i):
                    act.wait_ge(max_ready, b * TT + i + 1)
                    wait(act, t_full, b * TT + i - 1)
                    n = (i + 1) * P
                    act.activation(probs[:, i % 2, 0:n], s_bank[i % 2][:, 0:n], ACT.Exp,
                                   bias=neg_max[:, i % 2:i % 2 + 1]).then_inc(exp_done, 1)

                def turned(b, i):
                    act.wait_ge(t_full, b * TT + i + 1)
                    wait(act, o_full, b * TT + i - 1)
                    act.activation(probsT[:, i % 2, 0:i + 1, :], t_bank[:, 0:i + 1, :], ACT.Copy
                                   ).then_inc(turned_out, 1)

                for k in range(SHARED_USES):
                    shared_out(0, 0, k)

                def period(b, slot):
                    exps(b, 0)
                    for i in range(TT):
                        if i + 1 < TT:
                            exps(b, i + 1)
                        turned(b, i)
                        if has_next(b):
                            for k in USES_AT[i]:
                                shared_out(b + 1, 1 - slot, k)

                over_pairs_of_images(act, NB, period)

            @block.tensor
            def _(pe):
                pe.wait_ge(weights_in, 48)
                pe.matmul(shared[:, 0:P], wq[:], wk[:], start=True, stop=True).then_inc(wqk_mm, 1)
                pe.wait_ge(wqk_ready, 1)

                def shared_use(b, slot, k):
                    h = k % 2
                    wait(pe, shared_free, SHARED_USES * b + k)
                    if k == 0:
                        pe.wait_ge(staged_in, 16 * (b + 1))
                    if k == 2:
                        pe.wait_ge(e_ready, b + 1)
                    for n in range(TT // 2):
                        t = TT // 2 * h + n
                        out = shared[:, n * P:(n + 1) * P]
                        if k < 2:
                            last = pe.transpose(out, staged[:, t, :], ident[:])
                        elif k < 4:
                            last = pe.transpose(out, e_tok[:, t, :], ident[:])
                        elif k >= 6:
                            last = pe.matmul(out, eT[:, slot, t * P:(t + 1) * P], wvT[:], start=(n == 0),
                                             stop=(n == TT // 2 - 1), skip_group_check=True)
                    if 4 <= k < 6:
                        last = pe.matmul(shared[:], wqk[:], eT[:, slot, 512 * h:512 * (h + 1)], start=True, stop=True)
                    last.then_inc(shared_full, 1)

                def scores(b, slot, i):
                    if i == 0:
                        pe.wait_ge(shared_free, SHARED_USES * (b + 1))
                    wait(pe, masked, b * TT + i - 1)
                    for h in range(2):
                        last = pe.matmul(s_bank[i % 2][:, 512 * h:512 * (h + 1)], gT[:, slot, i * P:(i + 1) * P],
                                         eT[:, slot, 512 * h:512 * (h + 1)], start=True, stop=True)
                    last.then_inc(s_full, 1)

                def turn(b, i):
                    pe.wait_ge(masked, b * TT + i + 1)
                    wait(pe, turned_out, b * TT + i)
                    for t in range(i + 1):
                        last = pe.transpose(t_bank[:, t, :], probs[:, i % 2, t * P:(t + 1) * P], ident[:])
                    last.then_inc(t_full, 1)

                def values(b, slot, i):
                    pe.wait_ge(turned_out, b * TT + i + 1)
                    wait(pe, added, b * TT + i)
                    for t in range(i + 1):
                        last = pe.matmul(o_bank[:], probsT[:, i % 2, t, :], val[:, slot, t, :],
                                         start=(t == 0), stop=(t == i))
                    last.then_inc(o_full, 1)

                for k in range(SHARED_USES):
                    shared_use(0, 0, k)

                def period(b, slot):
                    scores(b, slot, 0)
                    for i in range(TT):
                        if i + 1 < TT:
                            scores(b, slot, i + 1)
                        turn(b, i)
                        if has_next(b):
                            for k in USES_AT[i]:
                                shared_use(b + 1, 1 - slot, k)
                        if i >= 1:
                            values(b, slot, i - 1)
                    values(b, slot, TT - 1)

                over_pairs_of_images(pe, NB, period)


USES_AT = [(0,), (1,), (), (), (2,), (3, 4), (5, 6), (7,)]


EXPERTS = 8
TOP = 2
HIDDEN = 341
GROUPS = TOP * EXPERTS
CHUNKS = 3
CHUNK = 114
ROW = 132
GATE, TOKEN = P, P + TOP
BIG = 3.0e38
DUMMIES = 8
F_BF = mybir.dt.bfloat16
I32 = mybir.dt.int32
U32 = mybir.dt.uint32


def route_tokens(nc, X, ident, table, routed, dram):
    NB = X.shape[1]
    NTOK = NB * HW
    REGION = NTOK + P
    TILES = NTOK // P + DUMMIES
    XT = X[:].rearrange("p b (t c) -> p b t c", c=P)
    with ExitStack() as ctx:
        def sb(name, shape, dt=F32):
            return ctx.enter_context(nc.sbuf_tensor("r_" + name, shape, dt))

        def ps(name, shape):
            return ctx.enter_context(nc.psum_tensor("r_" + name, shape, F32))

        def sem(name):
            return ctx.enter_context(nc.semaphore("r_" + name))

        minus_half = sb("minus_half", [P, TT])
        zero = sb("zero", [P, TT, TOP], I32)
        rwT = sb("rwT", [P, EXPERTS])
        ones = sb("ones", [P, P], F_BF)
        before = sb("before", [P, P], F_BF)
        expert_i = sb("expert_i", [P, TT, EXPERTS], I32)
        expert_no = sb("expert_no", [P, TT, EXPERTS])
        group_i = sb("group_i", [P, GROUPS], I32)
        group_row = sb("group_row", [P, GROUPS])
        next_row = sb("next_row", [P, 2, GROUPS])
        token_i = sb("token_i", [P, NB, TT], I32)
        pad = sb("pad", [P, ROW])
        lane_i = sb("lane_i", [P, GROUPS], I32)
        lane = sb("lane", [P, GROUPS])
        pad_row = sb("pad_row", [P, GROUPS])
        pad_idx = sb("pad_idx", [P, GROUPS], I32)
        ln_st = sb("ln_st", [P, TT, 6])
        ln_mv = sb("ln_mv", [P, TT, 2])
        ln_ve = sb("ln_ve", [P, TT])
        ln_rs = sb("ln_rs", [P, TT])
        rows = sb("rows", [P, 2, TT, ROW])
        eT = sb("eT", [P, HW])
        logits = sb("logits", [P, TT, EXPERTS])
        rest = sb("rest", [P, TT, EXPERTS])
        top = sb("top", [P, TOP, TT])
        below = sb("below", [P, TT, EXPERTS])
        numbered = sb("numbered", [P, TT, EXPERTS])
        chosen = sb("chosen", [P, TOP, TT])
        pick = sb("pick", [P, TOP, TT, EXPERTS])
        pick_bf = sb("pick_bf", [P, TT, TOP, EXPERTS], F_BF)
        ex_in = sb("ex_in", [P, TT, EXPERTS + 1])
        ex = sb("ex", [P, TT, EXPERTS + 1])
        ex_sum = sb("ex_sum", [P, TT])
        den0 = sb("den0", [P, TT])
        den = sb("den", [P, TT])
        gate0 = sb("gate0", [P, TT])
        place = sb("place", [P, TT, GROUPS])
        placed = sb("placed", [P, TT, GROUPS])
        target = sb("target", [P, TT, TOP])
        target_i = sb("target_i", [P, TT, TOP], I32)
        target_idx = sb("target_idx", [P, TT, TOP], I32)
        amount = sb("amount", [P, GROUPS])
        amount_i = sb("amount_i", [P, GROUPS], I32)
        ntiles_i = sb("ntiles_i", [P, GROUPS], I32)
        ntiles = sb("ntiles", [P, GROUPS])
        ends = sb("ends", [P, GROUPS])
        one_row = sb("one_row", [P, GROUPS])
        offset = sb("offset", [P, TOP, EXPERTS + 1])
        step_up = sb("step_up", [P, TOP, EXPERTS])
        tile_i = sb("tile_i", [1, TOP, TILES, EXPERTS], I32)
        tile_no = sb("tile_no", [1, TOP, TILES, EXPERTS])
        passed = sb("passed", [1, TOP, TILES, EXPERTS])
        jumps = sb("jumps", [1, TOP, TILES, EXPERTS])
        tile_sum = sb("tile_sum", [1, TOP, TILES])
        tile_row = sb("tile_row", [1, TOP, TILES])
        tile_expert = sb("tile_expert", [1, TOP, TILES])

        e_bank = ps("e_bank", [P, TT, P])
        l_bank = ps("l_bank", [P, TT, EXPERTS])
        p_bank = ps("p_bank", [P, TT + 1, GROUPS])

        names = ("weights_in const iotas casts ve rs mv norm e_full e_out l_full logits top0 below0 numbered0 chosen0 "
                 "pick0 rest top1 below1 numbered1 chosen1 pick1 ex_in gap ex ex_sum den0 den gate0 gates pick_bf "
                 "p_full next_row place placed target target_i idx scattered pads pad_idx_ready pad_row_ready amounts "
                 "table_step cleared pow_ready").split()
        s = {n: sem(n) for n in names}

        def has_next(b):
            return not (isinstance(b, int) and b == NB - 1)

        with nc.Block() as block:

            @block.sync
            def _(sp):
                sp.dma_start(rwT[:], dram["rwT"]).then_inc(s["weights_in"], 16)

            @block.gpsimd
            def _(pool):
                pool.memset(minus_half[:], -0.5)
                pool.memset(zero[:], 0)
                pool.memset(ones[:], 1.0)
                pool.memset(before[:], 1.0).then_inc(s["const"], 1)
                pool.wait_ge(s["const"], 1)
                pool.affine_select(out=before[:], in_=before[:], compare_op=ALU.is_gt, fill=0.0, base=0,
                                   pattern=[[1, P]], channel_multiplier=-1)
                pool.iota(expert_i[:], [[0, TT], [1, EXPERTS]], base=0, channel_multiplier=0)
                pool.iota(group_i[:], [[REGION // P, GROUPS]], base=0, channel_multiplier=0)
                pool.iota(token_i[:], [[HW, NB], [P, TT]], base=0, channel_multiplier=1)
                pool.iota(lane_i[:], [[0, GROUPS]], base=0, channel_multiplier=1)
                pool.iota(tile_i[:], [[0, TOP], [1, TILES], [0, EXPERTS]], base=0,
                          channel_multiplier=0).then_inc(s["iotas"], 1)

                def rsqrt(b):
                    pool.wait_ge(s["ve"], b + 1)
                    pool.tensor_tensor(ln_rs[:], ln_ve[:], minus_half[:], ALU.pow).then_inc(s["rs"], 1)

                rsqrt(0)

                def period(b, slot):
                    if has_next(b):
                        rsqrt(b + 1)
                    pool.wait_ge(s["gates"], b + 1)
                    wait(pool, s["scattered"], b * 16 * TT * TOP)
                    pool.wait_ge(s["target_i"], b + 1)
                    pool.tensor_tensor(target_idx[:], target_i[:], zero[:], ALU.add).then_inc(s["idx"], 1)
                    pool.drain()
                    for t in range(TT):
                        for k in range(TOP):
                            pool.indirect_dma_start(
                                out=routed, out_offset=bass.IndirectOffsetOnAxis(ap=target_idx[:, t, k:k + 1], axis=0),
                                in_=rows[:, slot, t, :], in_offset=None).then_inc(s["scattered"], 16)

                over_pairs_of_images(pool, NB, period)
                pool.wait_ge(s["pad_idx_ready"], 1)
                for g in range(GROUPS):
                    pool.indirect_dma_start(
                        out=routed, out_offset=bass.IndirectOffsetOnAxis(ap=pad_idx[:, g:g + 1], axis=0),
                        in_=pad[:], in_offset=None).then_inc(s["pads"], 16)
                for d in range(DUMMIES):
                    at = GROUPS * REGION + d * P
                    pool.dma_start(routed[at:at + P, :], pad[:]).then_inc(s["pads"], 16)
                pool.wait_ge(s["pads"], 16 * (GROUPS + DUMMIES))
                pool.wait_ge(s["scattered"], 16 * TT * TOP * NB)

            @block.vector
            def _(dve):
                def then(name, b, ins):
                    ins.then_inc(s[name], 1)
                    dve.wait_ge(s[name], b + 1)

                dve.memset(rows[:], 0.0)
                dve.memset(pad[:], 0.0)
                dve.memset(one_row[:], 1.0).then_inc(s["cleared"], 1)
                dve.wait_ge(s["cleared"], 1)
                dve.wait_ge(s["iotas"], 1)
                dve.tensor_copy(expert_no[:], expert_i[:])
                dve.tensor_copy(lane[:], lane_i[:])
                dve.tensor_copy(tile_no[:], tile_i[:])
                dve.tensor_scalar(group_row[:], group_i[:], float(P), None, ALU.mult)
                dve.tensor_scalar(next_row[:, 0, :], group_i[:], float(P), None, ALU.mult)
                dve.tensor_scalar(pad[:, TOKEN:TOKEN + 1].bitcast(I32), lane_i[:, 0:1], float(NTOK), None,
                                  ALU.add).then_inc(s["casts"], 1)
                dve.wait_ge(s["casts"], 1)

                def stats(b):
                    for t in range(TT):
                        dve.bn_stats(ln_st[:, t, :], XT[:, b, t, :])
                    dve.drain()
                    for t in range(TT):
                        last = dve.bn_aggr(ln_mv[:, t, :], ln_st[:, t, :])
                    then("mv", b, last)
                    dve.tensor_scalar(ln_ve[:], ln_mv[:, :, 1], LN_EPS, None, ALU.add).then_inc(s["ve"], 1)

                def norm(b, slot):
                    dve.wait_ge(s["rs"], b + 1)
                    wait(dve, s["scattered"], (b - 1) * 16 * TT * TOP)
                    for t in range(TT):
                        dve.tensor_scalar(rows[:, slot, t, 0:P], XT[:, b, t, :], ln_mv[:, t, 0:1],
                                          ln_rs[:, t:t + 1], ALU.subtract, ALU.mult)
                    dve.tensor_copy(rows[:, slot, :, TOKEN].bitcast(I32), token_i[:, b, :]).then_inc(s["norm"], 1)

                def per_tile(a):
                    return a.unsqueeze(2).to_broadcast([P, TT, EXPERTS])

                def choose(b, k, source):
                    then(f"top{k}", b, dve.tensor_reduce(top[:, k, :], source[:], AX_X, ALU.max))
                    then(f"below{k}", b, dve.tensor_tensor(below[:], source[:], per_tile(top[:, k, :]), ALU.is_lt))
                    then(f"numbered{k}", b, dve.scalar_tensor_tensor(
                        out=numbered[:], in0=below[:], scalar=float(EXPERTS), in1=expert_no[:],
                        op0=ALU.mult, op1=ALU.add))
                    then(f"chosen{k}", b, dve.tensor_reduce(chosen[:, k, :], numbered[:], AX_X, ALU.min))
                    then(f"pick{k}", b, dve.tensor_tensor(pick[:, k, :, :], expert_no[:], per_tile(chosen[:, k, :]),
                                                          ALU.is_equal))

                def route(b, slot, parity):
                    dve.wait_ge(s["l_full"], b + 1)
                    then("logits", b, dve.tensor_copy(logits[:], l_bank[:]))
                    choose(b, 0, logits)
                    then("rest", b, dve.scalar_tensor_tensor(
                        out=rest[:], in0=pick[:, 0, :, :], scalar=-BIG, in1=logits[:], op0=ALU.mult, op1=ALU.add))
                    choose(b, 1, rest)
                    dve.tensor_tensor(ex_in[:, :, 0:EXPERTS], logits[:], per_tile(top[:, 0, :]), ALU.subtract)
                    dve.tensor_tensor(ex_in[:, :, EXPERTS], top[:, 1, :], top[:, 0, :], ALU.subtract
                                      ).then_inc(s["ex_in"], 1)
                    wait(dve, s["p_full"], b)
                    dve.tensor_copy(pick_bf[:], pick[:].rearrange("p k t e -> p t k e")).then_inc(s["pick_bf"], 1)
                    dve.wait_ge(s["ex"], b + 1)
                    then("ex_sum", b, dve.tensor_reduce(ex_sum[:], ex[:, :, 0:EXPERTS], AX_X, ALU.add))
                    then("den0", b, dve.scalar_tensor_tensor(out=den0[:], in0=ex_sum[:], scalar=1e-9,
                                                             in1=ex[:, :, EXPERTS], op0=ALU.mult, op1=ALU.add))
                    then("den", b, dve.tensor_scalar(den[:], den0[:], 1.0, None, ALU.add))
                    then("gate0", b, dve.reciprocal(gate0[:], den[:]))
                    dve.tensor_copy(rows[:, slot, :, GATE], gate0[:])
                    dve.tensor_tensor(rows[:, slot, :, GATE + 1], gate0[:], ex[:, :, EXPERTS], ALU.mult
                                      ).then_inc(s["gates"], 1)
                    dve.wait_ge(s["p_full"], b + 1)
                    carry = next_row[:, parity, :]
                    dve.tensor_tensor(next_row[:, 1 - parity, :], carry, p_bank[:, TT, :], ALU.add)
                    then("place", b, dve.tensor_tensor(place[:], p_bank[:, 0:TT, :],
                                                       carry.unsqueeze(1).to_broadcast([P, TT, GROUPS]), ALU.add))
                    then("placed", b, dve.tensor_tensor(placed[:].rearrange("p t (k e) -> p t k e", k=TOP),
                                                        place[:].rearrange("p t (k e) -> p t k e", k=TOP),
                                                        pick_bf[:], ALU.mult))
                    then("target", b, dve.tensor_reduce(target[:], placed[:].rearrange("p t (k e) -> p t k e", k=TOP),
                                                        AX_X, ALU.add))
                    wait(dve, s["idx"], b)
                    dve.tensor_copy(target_i[:], target[:]).then_inc(s["target_i"], 1)

                stats(0)
                norm(0, 0)

                def period(b, slot):
                    if has_next(b):
                        stats(b + 1)
                        norm(b + 1, 1 - slot)
                    route(b, slot, slot)

                over_pairs_of_images(dve, NB, period)

                n = [0]

                def step(ins):
                    ins.then_inc(s["table_step"], 1)
                    n[0] += 1
                    dve.wait_ge(s["table_step"], n[0])

                final = next_row[:, NB % 2, :]
                step(dve.tensor_tensor(amount[:], final, group_row[:], ALU.subtract))
                step(dve.tensor_tensor(pad_row[:], final, lane[:], ALU.add))
                dve.tensor_copy(pad_idx[:], pad_row[:]).then_inc(s["pad_idx_ready"], 1)
                step(dve.tensor_scalar(amount_i[:], amount[:], float(P - 1), None, ALU.add))
                step(dve.tensor_scalar(ntiles_i[:], amount_i[:], P.bit_length() - 1, None, ALU.logical_shift_right))
                step(dve.tensor_copy(ntiles[:], ntiles_i[:]))
                for k in range(TOP):
                    g = slice(k * EXPERTS, (k + 1) * EXPERTS)
                    step(dve.tensor_tensor_scan(ends[:, g], one_row[:, g], ntiles[:, g], 0.0, ALU.mult, ALU.add))
                step(dve.tensor_tensor(amount[:], ends[:], ntiles[:], ALU.subtract))
                by_choice = lambda a: a[:].rearrange("p (k e) -> p k e", k=TOP)
                step(dve.scalar_tensor_tensor(out=offset[:, :, 0:EXPERTS], in0=by_choice(amount), scalar=-float(P),
                                              in1=by_choice(group_row), op0=ALU.mult, op1=ALU.add))
                step(dve.tensor_scalar(offset[:, :, EXPERTS], by_choice(ends)[:, :, EXPERTS - 1], -float(P),
                                       float(GROUPS * REGION), ALU.mult, ALU.add))
                step(dve.tensor_tensor(step_up[:], offset[:, :, 1:], offset[:, :, 0:EXPERTS], ALU.subtract))
                for k in range(TOP):
                    every = lambda a: a.unsqueeze(1).to_broadcast([1, TILES, EXPERTS])
                    step(dve.tensor_tensor(passed[:, k], tile_no[:, k], every(by_choice(ends)[0:1, k, :]), ALU.is_ge))
                    step(dve.tensor_tensor(jumps[:, k], passed[:, k], every(step_up[0:1, k, :]), ALU.mult))
                step(dve.tensor_reduce(tile_sum[:], jumps[:], AX_X, ALU.add))
                step(dve.scalar_tensor_tensor(out=tile_row[:], in0=tile_no[:, :, :, 0], scalar=float(P), in1=tile_sum[:],
                                              op0=ALU.mult, op1=ALU.add))
                step(dve.tensor_reduce(tile_expert[:], passed[:], AX_X, ALU.add))
                for k in range(TOP):
                    step(dve.tensor_scalar(table[:, 0, k * TILES:(k + 1) * TILES], tile_row[:, k, :], offset[0:1, k, 0:1], None, ALU.add))
                    step(dve.tensor_scalar(table[:, 1, k * TILES:(k + 1) * TILES], tile_expert[:, k, :], float(EXPERTS - 1), None, ALU.min))

            @block.scalar
            def _(act):
                def evacuate(b):
                    act.wait_ge(s["e_full"], b + 1)
                    wait(act, s["l_full"], b)
                    act.activation(eT[:].rearrange("p (t c) -> p t c", c=P), e_bank[:], ACT.Copy
                                   ).then_inc(s["e_out"], 1)

                evacuate(0)

                def period(b, slot):
                    if has_next(b):
                        evacuate(b + 1)
                    act.wait_ge(s["ex_in"], b + 1)
                    act.activation(ex[:], ex_in[:], ACT.Exp).then_inc(s["ex"], 1)

                over_pairs_of_images(act, NB, period)

            @block.tensor
            def _(pe):
                pe.wait_ge(s["weights_in"], 16)
                pe.wait_ge(s["iotas"], 1)

                def turn(b, slot):
                    pe.wait_ge(s["norm"], b + 1)
                    wait(pe, s["e_out"], b)
                    for t in range(TT):
                        last = pe.transpose(e_bank[:, t, :], rows[:, slot, t, 0:P], ident[:])
                    last.then_inc(s["e_full"], 1)

                def logit(b):
                    pe.wait_ge(s["e_out"], b + 1)
                    wait(pe, s["logits"], b)
                    for t in range(TT):
                        last = pe.matmul(l_bank[:, t, :], eT[:, t * P:(t + 1) * P], rwT[:], start=(t == 0),
                                         stop=(t == TT - 1), skip_group_check=True)
                    last.then_inc(s["l_full"], 1)

                turn(0, 0)
                logit(0)

                def period(b, slot):
                    if has_next(b):
                        turn(b + 1, 1 - slot)
                    wait(pe, s["place"], b)
                    pe.wait_ge(s["pick_bf"], b + 1)
                    pe.matmul(p_bank[:, 0:TT, :], before[:], pick_bf[:].rearrange("p t k e -> p (t k e)"),
                              start=True, stop=False, skip_group_check=True)
                    for t in range(TT):
                        later = TT - t
                        last = pe.matmul(p_bank[:, t + 1:, :], ones[:],
                                         pick_bf[:, t, :, :].rearrange("p k e -> p (k e)").unsqueeze(1)
                                         .to_broadcast([P, later, GROUPS]),
                                         start=False, stop=(t == TT - 1), skip_group_check=True)
                    last.then_inc(s["p_full"], 1)
                    if has_next(b):
                        logit(b + 1)

                over_pairs_of_images(pe, NB, period)


RING = 4


def expert_tiles(nc, table, routed, answers, ident, ntok, dram):
    TILES = ntok // P + DUMMIES
    ALL = TOP * TILES
    with ExitStack() as ctx:
        def sb(name, shape, dt=F32):
            return ctx.enter_context(nc.sbuf_tensor("f_" + name, shape, dt))

        def ps(name, shape):
            return ctx.enter_context(nc.psum_tensor("f_" + name, shape, F32))

        def sem(name):
            return ctx.enter_context(nc.semaphore("f_" + name))

        w1 = sb("w1", [P, EXPERTS * HIDDEN])
        w3 = sb("w3", [P, EXPERTS * HIDDEN])
        w2 = sb("w2", [CHUNK, EXPERTS, CHUNKS, P])
        zero = sb("zero", [P, 1], I32)
        rows = sb("rows", [P, RING, ROW])
        xT = sb("xT", [P, 2, P])
        silu = sb("silu", [P, 2, HIDDEN])
        hidden = sb("hidden", [P, 2, CHUNKS * CHUNK])
        hiddenT = sb("hiddenT", [CHUNK, 2, CHUNKS, P])
        y = sb("y", [P, RING, P])
        token = sb("token", [P, RING], I32)

        x_bank = ps("x_bank", [P, P])
        h1_bank = [ps(f"h1_bank{i}", [P, 512]) for i in range(2)]
        h3_bank = [ps(f"h3_bank{i}", [P, 512]) for i in range(2)]
        hT_bank = ps("hT_bank", [CHUNK, CHUNKS, P])
        y_bank = ps("y_bank", [P, P])

        weights_in = sem("weights_in")
        cleared = sem("cleared")
        zero_ready = sem("zero_ready")
        row_in = [sem(f"row_in{i}") for i in range(RING)]
        x_turned = sem("x_turned")
        x_out = sem("x_out")
        h_full = sem("h_full")
        silu_done = sem("silu_done")
        gated = sem("gated")
        h_turned = sem("h_turned")
        h_out = sem("h_out")
        y_full = sem("y_full")
        y_out = sem("y_out")
        token_read = sem("token_read")
        y_sent = [sem(f"y_sent{i}") for i in range(RING)]

        def over_tiles(eng, body):
            turns = TILES // RING

            def turn(q, k):
                for i in range(RING):
                    body(RING * q + i, q, i, k)

            turn(0, 0)
            turn(1, 0)
            with eng.Fori(2, turns) as q:
                turn(q, 0)
            with eng.Fori(turns, 2 * turns - 1) as q:
                turn(q, 1)
            turn(2 * turns - 1, 1)

        def first(n):
            return isinstance(n, int) and n == 0

        def last_one(n):
            return isinstance(n, int) and n == ALL - 1

        def entry(n):
            return slice(n, n + 1) if isinstance(n, int) else bass.ds(n, 1)

        with nc.Block() as block:

            @block.sync
            def _(sp):
                sp.dma_start(w1[:], dram["w1T"]).then_inc(weights_in, 16)
                sp.dma_start(w3[:], dram["w3T"]).then_inc(weights_in, 16)
                for j in range(CHUNKS):
                    n = min(CHUNK, HIDDEN - j * CHUNK)
                    sp.dma_start(w2[0:n, :, j, :], dram["w2T"][:, j * CHUNK:j * CHUNK + n, :]
                                 .rearrange("e h c -> h e c")).then_inc(weights_in, 16)

                def load(n, q, i, k):
                    row = sp.value_load(table[0:1, 0, entry(n)], min_val=0,
                                        max_val=GROUPS * (ntok + P) + (DUMMIES - 1) * P)
                    wait(sp, token_read, n - RING + 1)
                    sp.dma_start(rows[:, i, :], routed[bass.ds(row, P), :]).then_inc(row_in[i], 16)

                over_tiles(sp, load)

            @block.gpsimd
            def _(pool):
                pool.memset(zero[:], 0).then_inc(zero_ready, 1)
                pool.wait_ge(zero_ready, 1)

                def send(n, q, i, k):
                    pool.wait_ge(y_out, n + 1)
                    pool.tensor_tensor(token[:, i:i + 1], rows[:, i, TOKEN:TOKEN + 1].bitcast(I32), zero[:],
                                       ALU.add).then_inc(token_read, 1)
                    pool.drain()
                    pool.indirect_dma_start(
                        out=answers[k], out_offset=bass.IndirectOffsetOnAxis(ap=token[:, i:i + 1], axis=0),
                        in_=y[:, i, :], in_offset=None, bounds_check=ntok - 1, oob_is_err=False
                    ).then_inc(y_sent[i], 16)

                over_tiles(pool, send)
                for i in range(RING):
                    pool.wait_ge(y_sent[i], 16 * (ALL // RING))

            @block.scalar
            def _(act):
                def x_evacuate(n, slot):
                    act.wait_ge(x_turned, n + 1)
                    wait(act, h_full, n - 1)
                    act.activation(xT[:, slot, :], x_bank[:], ACT.Copy).then_inc(x_out, 1)

                def h_evacuate(n, slot):
                    act.wait_ge(h_turned, n + 1)
                    wait(act, y_full, n - 1)
                    act.activation(hiddenT[:, slot, :, :], hT_bank[:], ACT.Copy).then_inc(h_out, 1)

                def body(n, q, i, k):
                    if first(n):
                        x_evacuate(0, 0)
                    if not last_one(n):
                        x_evacuate(n + 1, (i + 1) % 2)
                    if not first(n):
                        h_evacuate(n - 1, (i + 1) % 2)
                    act.wait_ge(h_full, n + 1)
                    wait(act, gated, n - 1)
                    act.activation(silu[:, i % 2, :], h1_bank[i % 2][:, 0:HIDDEN], ACT.Silu).then_inc(silu_done, 1)

                over_tiles(act, body)
                h_evacuate(ALL - 1, 1)

            @block.vector
            def _(dve):
                dve.memset(hidden[:], 0.0).then_inc(cleared, 1)
                dve.wait_ge(cleared, 1)

                def y_evacuate(n, q, i):
                    dve.wait_ge(y_full, n + 1)
                    wait(dve, y_sent[i], 16 * q)
                    dve.tensor_copy(y[:, i, :], y_bank[:]).then_inc(y_out, 1)

                def body(n, q, i, k):
                    dve.wait_ge(silu_done, n + 1)
                    wait(dve, h_turned, n - 1)
                    dve.scalar_tensor_tensor(out=hidden[:, i % 2, 0:HIDDEN], in0=silu[:, i % 2, :],
                                             scalar=rows[:, i, GATE + k:GATE + k + 1], in1=h3_bank[i % 2][:, 0:HIDDEN],
                                             op0=ALU.mult, op1=ALU.mult).then_inc(gated, 1)
                    if not first(n):
                        y_evacuate(n - 1, q - (i == 0), (i - 1) % RING)

                over_tiles(dve, body)
                y_evacuate(ALL - 1, ALL // RING - 1, RING - 1)

            @block.tensor
            def _(pe):
                pe.wait_ge(weights_in, 16 * (2 + CHUNKS))

                def turn_rows(n, q, i):
                    pe.wait_ge(row_in[i], 16 * (q + 1))
                    wait(pe, x_out, n)
                    pe.transpose(x_bank[:], rows[:, i, 0:P], ident[:]).then_inc(x_turned, 1)

                def up(n, i):
                    e = pe.value_load(table[0:1, 1, entry(n)], min_val=0, max_val=EXPERTS - 1)
                    pe.wait_ge(x_out, n + 1)
                    wait(pe, gated, n - 1)
                    pe.matmul(h1_bank[i % 2][:, 0:HIDDEN], xT[:, i % 2, :], w1[:, bass.ds(e * HIDDEN, HIDDEN)],
                              start=True, stop=True)
                    pe.matmul(h3_bank[i % 2][:, 0:HIDDEN], xT[:, i % 2, :], w3[:, bass.ds(e * HIDDEN, HIDDEN)],
                              start=True, stop=True).then_inc(h_full, 1)

                def turn_hidden(n, slot):
                    pe.wait_ge(gated, n + 1)
                    wait(pe, h_out, n)
                    for j in range(CHUNKS):
                        last = pe.transpose(hT_bank[:, j, :], hidden[:, slot, j * CHUNK:(j + 1) * CHUNK], ident[:])
                    last.then_inc(h_turned, 1)

                def down(n, slot):
                    e = pe.value_load(table[0:1, 1, entry(n)], min_val=0, max_val=EXPERTS - 1)
                    pe.wait_ge(h_out, n + 1)
                    wait(pe, y_out, n)
                    for j in range(CHUNKS):
                        m = min(CHUNK, HIDDEN - j * CHUNK)
                        last = pe.matmul(y_bank[:], hiddenT[0:m, slot, j, :], w2[0:m, bass.ds(e, 1), j, :],
                                         start=(j == 0), stop=(j == CHUNKS - 1))
                    last.then_inc(y_full, 1)

                def body(n, q, i, k):
                    if first(n):
                        turn_rows(0, 0, 0)
                    if not last_one(n):
                        turn_rows(n + 1, q + (i == RING - 1), (i + 1) % RING)
                    if not first(n):
                        turn_hidden(n - 1, (i + 1) % 2)
                    up(n, i)
                    if not first(n):
                        down(n - 1, (i + 1) % 2)

                over_tiles(pe, body)
                turn_hidden(ALL - 1, 1)
                down(ALL - 1, 1)


def add_answers(nc, X, answers, out):
    NB = X.shape[1]
    XT = X[:].rearrange("p b (t c) -> p b t c", c=P)
    with ExitStack() as ctx:
        parts = ctx.enter_context(nc.sbuf_tensor("parts", [P, 2, TOP, TT, P], F32))
        loaded = [ctx.enter_context(nc.semaphore(f"answers_in{i}")) for i in range(2)]
        summed = ctx.enter_context(nc.semaphore("summed"))
        first_added = ctx.enter_context(nc.semaphore("first_added"))
        stored = ctx.enter_context(nc.semaphore("stored"))
        with nc.Block() as block:

            @block.sync
            def _(sp):
                def load(b, slot):
                    for k in range(TOP):
                        rows = answers[k][bass.ds(b * HW, HW), :] if not isinstance(b, int) else \
                            answers[k][b * HW:(b + 1) * HW, :]
                        sp.dma_start(parts[:, slot, k, :, :], rows.rearrange("(t p) c -> p t c", p=P)
                                     ).then_inc(loaded[slot], 16)

                load(0, 0)
                load(1, 1)
                with sp.Fori(1, NB // 2) as pair:
                    for slot in range(2):
                        sp.wait_ge(summed, 2 * pair + slot - 1)
                        load(2 * pair + slot, slot)

            @block.vector
            def _(dve):
                for b in range(NB):
                    slot = b % 2
                    dve.wait_ge(loaded[slot], 16 * TOP * (b // 2 + 1))
                    dve.tensor_tensor(XT[:, b], XT[:, b], parts[:, slot, 0], ALU.add).then_inc(first_added, 1)
                    dve.wait_ge(first_added, b + 1)
                    dve.tensor_tensor(XT[:, b], XT[:, b], parts[:, slot, 1], ALU.add).then_inc(summed, 1)

            @block.scalar
            def _(act):
                for b in range(NB):
                    act.wait_ge(summed, b + 1)
                    act.dma_start(out[b].rearrange("(t p) c -> p t c", p=P), XT[:, b]).then_inc(stored, 16)
                act.wait_ge(stored, 16 * NB)


def build(nc, dram, out):
    NB = dram["x"].shape[0]
    ntok = NB * HW
    routed = nc.dram_tensor("routed", (GROUPS * (ntok + P) + DUMMIES * P, ROW), F32).ap()
    answers = [nc.dram_tensor(f"answers{k}", (ntok, P), F32).ap() for k in range(TOP)]
    with ExitStack() as ctx:
        X = ctx.enter_context(nc.sbuf_tensor("X", [P, NB, HW], F32))
        ident = ctx.enter_context(nc.sbuf_tensor("ident", [P, P], F32))
        table = ctx.enter_context(nc.sbuf_tensor("table", [1, 2, TOP * (ntok // P + DUMMIES)], I32))
        conv_attention(nc, X, ident, dram)
        causal_attention(nc, X, ident, dram)
        route_tokens(nc, X, ident, table, routed, dram)
        expert_tiles(nc, table, routed, answers, ident, ntok, dram)
        add_answers(nc, X, answers, out)


def kernel(**inputs):
    import numpy as _np
    import concourse.bacc as _bacc
    from concourse import mybir as _mybir
    from concourse.bass_utils import run_bass_kernel_spmd as _run

    x = _np.asarray(inputs["x"])
    B, C, H, W = x.shape
    get = lambda n: _np.asarray(inputs[n])
    laid = {
        "x": x.reshape(B, C, H * W),
        "qWT": get("L0_conv_qW").T, "kWT": get("L0_conv_kW").T, "vWT": get("L0_conv_vW").T,
        "oWT": get("L0_conv_oW").T,
        "kdw": get("L0_conv_kdwW").reshape(C, 9), "vdw": get("L0_conv_vdwW").reshape(C, 9),
        "bn": _np.stack([_np.stack([get(f"L0_conv_{s}dw_{n}") for s in "kv"], 1)
                         for n in ("gamma", "beta", "mean", "var")], 1),
    }
    laid.update(wq=get("L1_attn_WQ"), wk=get("L1_attn_WK"), wvT=get("L1_attn_WV").T)
    hidden_first = lambda n: get(n).transpose(2, 0, 1).reshape(C, -1)
    laid.update(rwT=get("L1_ffn_router_w").T, w1T=hidden_first("L1_ffn_w1"), w3T=hidden_first("L1_ffn_w3"),
                w2T=get("L1_ffn_w2").transpose(0, 2, 1))
    nc = _bacc.Bacc("TRN2", target_bir_lowering=False, num_devices=1)
    arrays, dram = {}, {}
    for name, a in laid.items():
        a = _np.ascontiguousarray(a)
        arrays[f"in_{name}"] = a
        dram[name] = nc.dram_tensor(f"in_{name}", a.shape, _mybir.dt.from_np(a.dtype), kind="ExternalInput").ap()
    out = nc.dram_tensor("out_0", (B, H * W, C), _mybir.dt.float32, kind="ExternalOutput").ap()
    build(nc, dram, out)
    r = _run(nc, [arrays], core_ids=[0])
    return r.results[0]["out_0"].reshape(B, H, W, C).transpose(0, 3, 1, 2)
```

```python
from contextlib import ExitStack

import concourse.bass as bass
from concourse import mybir

ALU = mybir.AluOpType
ACT = mybir.ActivationFunctionType
AX_X = mybir.AxisListType.X
F32 = mybir.dt.float32
F32R = mybir.dt.float32r

P = 128
HW = 1024
SIDE = 32
CP = 256
CT = CP // P
KD = 32
L = 256
LT = L // P
ROWS = SIDE
PAIRS = ROWS // 2
TAPS = 9
GN_GROUP = 4
GN_EPS = 1e-5
BN_EPS = 1e-5
COPIES = 3
STACK = COPIES * KD
TURN = 66
Q_CHUNKS = 4
FRONT_USES = 3 + Q_CHUNKS
Q_STEPS = (7, 9, 12, 15)
OUT_USES = 2


def wait(eng, sem, value):
    if isinstance(value, int) and value <= 0:
        return
    eng.wait_ge(sem, value)


def over_images(eng, n, period):
    period(0)
    with eng.Fori(1, n - 1) as b:
        period(b)
    period(n - 1)
    period(n)


def conv_attention(nc, X, ident, dram):
    NB = X.shape[1]
    with ExitStack() as ctx:
        def sb(name, shape, dt=F32):
            return ctx.enter_context(nc.sbuf_tensor(name, shape, dt))

        def ps(name, shape):
            return ctx.enter_context(nc.psum_tensor(name, shape, F32))

        def sem(name):
            return ctx.enter_context(nc.semaphore(name))

        group_mean = sb("group_mean", [P, P])
        minus_half = sb("minus_half", [P, 2])
        qwT = sb("qwT", [P, CP])
        kwT = sb("kwT", [P, KD])
        vwT = sb("vwT", [P, KD])
        owT = sb("owT", [P, CT, P])
        kdw = sb("kdw", [P, TAPS])
        vdw = sb("vdw", [P, TAPS])
        bn = sb("bn", [P, 4, 2])
        bn_ve = sb("bn_ve", [P, 2])
        bn_rs = sb("bn_rs", [P, 2])
        bn_scale = sb("bn_scale", [P, 2])
        bn_ms = sb("bn_ms", [P, 2])
        bn_shift = sb("bn_shift", [P, 2])
        tap_scale = sb("tap_scale", [P, 2, TAPS])
        kv_w = sb("kv_w", [P, P])
        tap_w = sb("tap_w", [P, TAPS, P])
        kv_bias = sb("kv_bias", [P, 1])
        xn = sb("xn", [P, SIDE, SIDE])
        bn_st = sb("bn_st", [P, 2, 6])
        mv = sb("mv", [P, 2])
        dmean = sb("dmean", [P, 1])
        gmean = sb("gmean", [P, 1])
        spread = sb("spread", [P, 1])
        gvar = sb("gvar", [P, 1])
        grs = sb("grs", [P, 1])
        kv = sb("kv", [P, L])
        k_high = sb("k_high", [P, L], F32R)
        k_stack = sb("k_stack", [STACK, L], F32R)
        v_flat = sb("v_flat", [P, L])
        v_next = sb("v_next", [P, LT, KD])
        v_ones = sb("v_ones", [P, LT, KD + 1])
        q_high = sb("q_high", [P, ROWS // 4, CP], F32R)
        q_low = sb("q_low", [P, ROWS // 4, CP], F32R)
        q_stack = sb("q_stack", [STACK, ROWS, CP], F32R)
        neg_max = sb("neg_max", [P, ROWS, CT])
        probs = sb("probs", [P, 2, CT, L])
        probsT = sb("probsT", [P, 2, LT, 2, CP])
        ctxT = sb("ctxT", [TURN, 2, 2 * CP])
        rsum = sb("rsum", [P, 2, 4])
        context = sb("context", [P, CT, ROWS, KD])

        s_bank = [ps(f"s_bank{i}", [P, CT, L]) for i in range(2)]
        t_bank = [ps(f"t_bank{i}", [P, LT, CP]) for i in range(2)]
        o_bank = ps("o_bank", [P, 2 * CP])
        c_bank = ps("c_bank", [P, 4, TURN])
        front = ps("front", [P, 512])

        weights_in = sem("weights_in")
        first_in = sem("first_in")
        rest_in = sem("rest_in")
        consts = sem("consts")
        bn_eps_added = sem("bn_eps_added")
        bn_rsqrt = sem("bn_rsqrt")
        setup_step = sem("setup_step")
        weights_ready = sem("weights_ready")
        bias_mm = sem("bias_mm")
        bias_ready = sem("bias_ready")
        chan_stats_ready = sem("chan_stats_ready")
        gmean_ready = sem("gmean_ready")
        dmean_ready = sem("dmean_ready")
        spread_ready = sem("spread_ready")
        k_high_ready = sem("k_high_ready")
        rsum_ready = sem("rsum_ready")
        gvar_ready = sem("gvar_ready")
        grs_ready = sem("grs_ready")
        xn_ready = sem("xn_ready")
        front_full = sem("front_full")
        kv_ready = sem("kv_ready")
        k_ready = sem("k_ready")
        v_staged = sem("v_staged")
        v_in = sem("v_in")
        v_ready = sem("v_ready")
        q_high_done = sem("q_high_done")
        q_low_done = sem("q_low_done")
        q_in = [sem(f"q_in{k}") for k in range(Q_CHUNKS)]
        s_full = sem("s_full")
        max_ready = sem("max_ready")
        probs_full = sem("probs_full")
        t_full = sem("t_full")
        evac_even = sem("evac_even")
        evac_odd = sem("evac_odd")
        o_full = sem("o_full")
        ctxT_full = sem("ctxT_full")
        c_full = sem("c_full")
        ctx_done = sem("ctx_done")
        out_done = sem("out_done")

        N_WEIGHTS = 7
        Q_IN = 16 * COPIES * 4
        USES = FRONT_USES + OUT_USES

        def before_period(b):
            return FRONT_USES + (USES - 1) + USES * (b - 1)

        def front_count(b, k):
            first_projection = int(k == FRONT_USES - 1)
            if isinstance(b, int) and b == 0:
                return k
            if isinstance(b, int) and b == 1:
                return FRONT_USES + k + first_projection
            return before_period(b - 1) + k + (k >= 2) + first_projection

        def out_count(b, k):
            if k == 0:
                if isinstance(b, int) and b == 0:
                    return 2 * FRONT_USES - 1
                return before_period(b) + (1 if isinstance(b, int) and b == NB - 1 else FRONT_USES)
            if isinstance(b, int) and b == NB - 1:
                return before_period(b) + 2
            return before_period(b + 1) + (0 if isinstance(b, int) and b == NB - 2 else 2)

        def has(b):
            return not isinstance(b, int) or 0 <= b < NB

        def pair(b, p):
            return (b, p) if p >= 0 else (b - 1, p + PAIRS)

        with nc.Block() as block:

            @block.sync
            def _(sp):
                sp.dma_start(X[:, 0, :], dram["x"][0]).then_inc(first_in, 16)
                for tile, src in ((qwT, dram["qWT"]), (kwT, dram["kWT"]), (vwT, dram["vWT"]),
                                  (kdw, dram["kdw"]), (vdw, dram["vdw"])):
                    sp.dma_start(tile[:], src).then_inc(weights_in, 16)
                sp.dma_start(owT[:], dram["oWT"].rearrange("(t p) o -> p t o", p=P)).then_inc(weights_in, 16)
                sp.dma_start(bn[:], dram["bn"]).then_inc(weights_in, 16)
                sp.dma_start(X[:, 1:, :], dram["x"][1:].rearrange("b p n -> p b n")).then_inc(rest_in, 16)

                def stack(b):
                    sp.wait_ge(v_staged, b + 1)
                    for t in range(LT):
                        sp.dma_start(v_next[:, t, :],
                                     v_flat[STACK + 16 * t:STACK + 16 * (t + 1), :]).then_inc(v_in, 16)
                    for k in range(Q_CHUNKS):
                        sp.wait_ge(q_low_done, Q_CHUNKS * b + k + 1)
                        for r, part in enumerate((q_high, q_low, q_high)):
                            for j in range(4):
                                sp.dma_start(q_stack[r * KD:(r + 1) * KD, 8 * k + j:8 * (k + 1):4, :].bitcast(F32),
                                             part[j * KD:(j + 1) * KD, 2 * k:2 * k + 2, :].bitcast(F32)
                                             ).then_inc(q_in[k], 16)

                stack(0)
                if NB > 1:
                    with sp.Fori(1, NB) as b:
                        stack(b)

            @block.gpsimd
            def _(pool):
                pool.memset(minus_half[:], -0.5).then_inc(consts, 1)
                pool.memset(ident[:], 0.0).then_inc(consts, 1)
                pool.memset(group_mean[:], 1.0 / GN_GROUP).then_inc(consts, 1)
                pool.wait_ge(consts, 3)
                pool.affine_select(out=ident[:], in_=ident[:], compare_op=ALU.not_equal, fill=1.0, base=0,
                                   pattern=[[-1, P]], channel_multiplier=1).then_inc(consts, 1)
                blocks = group_mean[:].rearrange("p (g i) -> p g i", i=GN_GROUP)
                pool.affine_select(out=blocks, in_=blocks, compare_op=ALU.is_ge, fill=0.0, base=0,
                                   pattern=[[-GN_GROUP, P // GN_GROUP], [0, GN_GROUP]],
                                   channel_multiplier=1).then_inc(consts, 1)
                pool.wait_ge(consts, 5)
                pool.affine_select(out=blocks, in_=blocks, compare_op=ALU.is_ge, fill=0.0, base=GN_GROUP - 1,
                                   pattern=[[GN_GROUP, P // GN_GROUP], [0, GN_GROUP]],
                                   channel_multiplier=-1).then_inc(consts, 1)
                pool.wait_ge(bn_eps_added, 1)
                pool.tensor_tensor(bn_rs[:], bn_ve[:], minus_half[:], ALU.pow).then_inc(bn_rsqrt, 1)
                with pool.Fori(0, NB) as b:
                    pool.wait_ge(gvar_ready, b + 1)
                    pool.tensor_tensor(grs[:], gvar[:], minus_half[:, 0:1], ALU.pow).then_inc(grs_ready, 1)

            @block.vector
            def _(dve):
                steps = [0]

                def link(ins):
                    ins.then_inc(setup_step, 1)
                    steps[0] += 1
                    dve.wait_ge(setup_step, steps[0])

                dve.memset(v_ones[:, :, KD:KD + 1], 1.0)
                dve.memset(ctxT[:], 0.0).then_inc(weights_ready, 1)
                dve.wait_ge(weights_in, 16 * N_WEIGHTS)
                gamma, beta, mean, var = (bn[:, i, :] for i in range(4))
                dve.tensor_scalar(bn_ve[:], var, BN_EPS, None, ALU.add).then_inc(bn_eps_added, 1)
                for r in range(COPIES):
                    link(dve.tensor_scalar(kv_w[:, r * KD:(r + 1) * KD], kwT[:], 0.5, None, ALU.mult))
                link(dve.tensor_copy(kv_w[:, STACK:], vwT[:]))
                dve.wait_ge(bn_rsqrt, 1)
                link(dve.tensor_tensor(bn_scale[:], gamma, bn_rs[:], ALU.mult))
                link(dve.tensor_tensor(bn_ms[:], mean, bn_scale[:], ALU.mult))
                link(dve.tensor_tensor(bn_shift[:], beta, bn_ms[:], ALU.subtract))
                link(dve.tensor_scalar(tap_scale[:, 0, :], kdw[:], bn_scale[:, 0:1], None, ALU.mult))
                link(dve.tensor_scalar(tap_scale[:, 1, :], vdw[:], bn_scale[:, 1:2], None, ALU.mult))
                for t in range(TAPS):
                    dve.tensor_scalar(tap_w[:, t, 0:STACK], kv_w[:, 0:STACK], tap_scale[:, 0, t:t + 1], None, ALU.mult)
                    last = dve.tensor_scalar(tap_w[:, t, STACK:], kv_w[:, STACK:], tap_scale[:, 1, t:t + 1], None,
                                             ALU.mult)
                last.then_inc(weights_ready, 1)
                dve.wait_ge(bias_mm, 1)
                dve.tensor_copy(kv_bias[0:STACK, :], front[0:STACK, 0:1]).then_inc(bias_ready, 1)
                dve.tensor_copy(kv_bias[STACK:, :], front[STACK:, 1:2]).then_inc(bias_ready, 1)
                dve.wait_ge(bias_ready, 2)

                def channel_stats(b):
                    for i in range(2):
                        dve.bn_stats(bn_st[:, i, :], X[:, b, 512 * i:512 * (i + 1)])
                    dve.drain()
                    dve.bn_aggr(mv[:], bn_st[:]).then_inc(chan_stats_ready, 1)

                def group_spread(b):
                    dve.wait_ge(front_full, front_count(b, 0) + 1)
                    dve.tensor_copy(gmean[:], front[:, 0:1]).then_inc(gmean_ready, 1)
                    dve.wait_ge(gmean_ready, b + 1)
                    dve.tensor_tensor(dmean[:], mv[:, 0:1], gmean[:], ALU.subtract).then_inc(dmean_ready, 1)
                    dve.wait_ge(dmean_ready, b + 1)
                    dve.scalar_tensor_tensor(out=spread[:], in0=dmean[:], scalar=dmean[:], in1=mv[:, 1:2],
                                             op0=ALU.mult, op1=ALU.add).then_inc(spread_ready, 1)

                def group_variance(b):
                    dve.wait_ge(front_full, front_count(b, 1) + 1)
                    dve.tensor_scalar(gvar[:], front[:, 1:2], GN_EPS, None, ALU.add).then_inc(gvar_ready, 1)

                def group_norm(b):
                    dve.wait_ge(grs_ready, b + 1)
                    dve.tensor_scalar(xn[:].rearrange("p h w -> p (h w)"), X[:, b, :], gmean[:], grs[:],
                                      ALU.subtract, ALU.mult).then_inc(xn_ready, 1)

                def keys_values(b):
                    dve.wait_ge(front_full, front_count(b, 2) + 1)
                    dve.tensor_scalar(kv[:], front[:, 0:L], kv_bias[:], None, ALU.add).then_inc(kv_ready, 1)

                def split_keys(b):
                    dve.wait_ge(kv_ready, b + 1)
                    wait(dve, s_full, b * ROWS)
                    dve.tensor_copy(k_stack[0:2 * KD, :], kv[0:2 * KD, :])
                    dve.tensor_copy(k_high[2 * KD:STACK, :], kv[2 * KD:STACK, :]).then_inc(k_high_ready, 1)
                    dve.wait_ge(k_high_ready, b + 1)
                    dve.tensor_tensor(k_stack[2 * KD:STACK, :], kv[2 * KD:STACK, :],
                                      k_high[2 * KD:STACK, :].bitcast(F32), ALU.subtract).then_inc(k_ready, 1)

                def stage_values(b):
                    wait(dve, v_in, b * 16 * LT)
                    dve.tensor_copy(v_flat[STACK:, :], kv[STACK:, :]).then_inc(v_staged, 1)

                def take_values(b):
                    dve.wait_ge(v_in, (b + 1) * 16 * LT)
                    wait(dve, o_full, b * PAIRS)
                    dve.tensor_copy(v_ones[:, :, 0:KD], v_next[:]).then_inc(v_ready, 1)

                def query_low(b, k):
                    dve.wait_ge(q_high_done, Q_CHUNKS * b + k + 1)
                    wait(dve, q_in[k], b * Q_IN)
                    dve.tensor_tensor(q_low[:, 2 * k:2 * k + 2, :],
                                      front[:].rearrange("p (g c) -> p g c", c=CP),
                                      q_high[:, 2 * k:2 * k + 2, :].bitcast(F32),
                                      ALU.subtract).then_inc(q_low_done, 1)

                def row_max(b, h):
                    dve.wait_ge(s_full, b * ROWS + h + 1)
                    dve.tensor_reduce(neg_max[:, h, :], s_bank[h % 2][:], AX_X, ALU.max,
                                      negate=True).then_inc(max_ready, 1)

                def evacuate_even(b, p):
                    dve.wait_ge(t_full, b * ROWS + 2 * p + 1)
                    wait(dve, o_full, b * PAIRS + p - 1)
                    dve.tensor_copy(probsT[:, p % 2, :, 0, :], t_bank[0][:]).then_inc(evac_even, 1)

                def normalise(b, p):
                    if p in (0, PAIRS // 2):
                        wait(dve, out_done, OUT_USES * b - (p == 0))
                    dve.wait_ge(c_full, b * PAIRS + p + 1)
                    dve.reciprocal(rsum[:, p % 2, :], c_bank[:, :, KD]).then_inc(rsum_ready, 1)
                    dve.wait_ge(rsum_ready, b * PAIRS + p + 1)
                    dve.tensor_tensor(context[:, :, 2 * p:2 * p + 2, :].rearrange("p t h d -> p h t d"),
                                      c_bank[:, :, 0:KD].rearrange("p (h t) d -> p h t d", t=CT),
                                      rsum[:, p % 2, :].rearrange("p (h t) -> p h t", t=CT).unsqueeze(3)
                                      .to_broadcast([P, 2, CT, KD]), ALU.mult).then_inc(ctx_done, 1)

                def add_output(b, k):
                    dve.wait_ge(front_full, out_count(b, k) + 1)
                    half = X[:, b, 512 * k:512 * (k + 1)]
                    dve.tensor_tensor(half, half, front[:], ALU.add).then_inc(out_done, 1)

                dve.wait_ge(first_in, 16)
                channel_stats(0)
                group_spread(0)
                group_variance(0)
                group_norm(0)
                keys_values(0)
                split_keys(0)
                stage_values(0)
                for k in range(Q_CHUNKS):
                    query_low(0, k)
                if NB > 1:
                    dve.wait_ge(rest_in, 16)

                def period(b):
                    nxt = has(b + 1)
                    for i in range(PAIRS if has(b) else 4):
                        if has(b):
                            row_max(b, 2 * i)
                            row_max(b, 2 * i + 1)
                        if nxt and i == PAIRS - 1:
                            split_keys(b + 1)
                        if i == 1 and has(b):
                            take_values(b)
                        if has(pair(b, i - 1)[0]):
                            evacuate_even(*pair(b, i - 1))
                        if has(pair(b, i - 3)[0]):
                            normalise(*pair(b, i - 3))
                        if nxt:
                            if i == 0:
                                channel_stats(b + 1)
                            if i == 1:
                                group_spread(b + 1)
                            if i == 2:
                                group_variance(b + 1)
                            if i == 3:
                                group_norm(b + 1)
                            if i == 5:
                                keys_values(b + 1)
                            if i == 6:
                                stage_values(b + 1)
                            if i in Q_STEPS:
                                query_low(b + 1, Q_STEPS.index(i))
                        if i == 3 and has(b - 1):
                            add_output(b - 1, 1)
                        if i == 13:
                            add_output(b, 0)

                over_images(dve, NB, period)

            @block.scalar
            def _(act):
                def query_high(b, k):
                    act.wait_ge(front_full, front_count(b, 3 + k) + 1)
                    wait(act, q_in[k], b * Q_IN)
                    act.activation(q_high[:, 2 * k:2 * k + 2, :], front[:].rearrange("p (g c) -> p g c", c=CP),
                                   ACT.Copy).then_inc(q_high_done, 1)

                def exps(b, h):
                    act.wait_ge(max_ready, b * ROWS + h + 1)
                    wait(act, t_full, b * ROWS + h - 1)
                    for t in range(CT):
                        last = act.activation(probs[:, h % 2, t, :], s_bank[h % 2][:, t, :], ACT.Exp,
                                              bias=neg_max[:, h, t:t + 1])
                    last.then_inc(probs_full, 1)

                def evacuate_odd(b, p):
                    act.wait_ge(t_full, b * ROWS + 2 * p + 2)
                    wait(act, o_full, b * PAIRS + p - 1)
                    act.activation(probsT[:, p % 2, :, 1, :], t_bank[1][:], ACT.Copy).then_inc(evac_odd, 1)

                def evacuate_context(b, p):
                    act.wait_ge(o_full, b * PAIRS + p + 1)
                    wait(act, c_full, b * PAIRS + p - 1)
                    act.activation(ctxT[0:KD + 1, p % 2, :], o_bank[0:KD + 1, :], ACT.Copy).then_inc(ctxT_full, 1)

                for k in range(Q_CHUNKS):
                    query_high(0, k)
                act.wait_ge(weights_ready, 2)

                def period(b):
                    for i in range(PAIRS if has(b) else 2):
                        if has(b):
                            exps(b, 2 * i)
                            exps(b, 2 * i + 1)
                        if has(pair(b, i - 1)[0]):
                            evacuate_odd(*pair(b, i - 1))
                        if has(pair(b, i - 2)[0]):
                            evacuate_context(*pair(b, i - 2))
                        if has(b + 1) and i in Q_STEPS:
                            query_high(b + 1, Q_STEPS.index(i))

                over_images(act, NB, period)

            @block.tensor
            def _(pe):
                pe.wait_ge(weights_in, 16 * N_WEIGHTS)
                pe.wait_ge(weights_ready, 2)
                pe.wait_ge(consts, 6)
                pe.matmul(front[:, 0:2], kv_w[:], bn_shift[:], start=True, stop=True).then_inc(bias_mm, 1)
                pe.wait_ge(bias_ready, 2)

                def group_sum(b, k, ready, column):
                    pe.wait_ge(ready, b + 1)
                    pe.matmul(front[:, k:k + 1], group_mean[:], column, start=True, stop=True).then_inc(front_full, 1)

                def keys_values(b):
                    pe.wait_ge(xn_ready, b + 1)
                    pe.wait_ge(gvar_ready, b + 1)
                    wait(pe, out_done, OUT_USES * (b - 1))
                    out = front[:, 0:L].rearrange("p (i j) -> p i j", j=SIDE // 2)
                    for n, t in enumerate((4, 0, 1, 2, 3, 5, 6, 7, 8)):
                        di, dj = divmod(t, 3)
                        last = pe.matmul(out[:, di == 0:, dj == 0:], tap_w[:, t, :],
                                         xn[:, (1, 0, 1)[di]:SIDE - (di == 0):2, (1, 0, 1)[dj]:SIDE - (dj == 0):2],
                                         start=(n == 0), stop=(n == TAPS - 1), skip_group_check=True)
                    last.then_inc(front_full, 1)

                def queries(b, k):
                    if k == 0:
                        pe.wait_ge(kv_ready, b + 1)
                    elif k < Q_CHUNKS - 1:
                        pe.wait_ge(q_low_done, Q_CHUNKS * b + k)
                    else:
                        pe.wait_ge(q_low_done, Q_CHUNKS * b + k)
                        wait(pe, out_done, OUT_USES * (b - 1) + 1)
                    for i in range(2):
                        g = 2 * k + i
                        last = pe.matmul(front[:, i * CP:(i + 1) * CP], xn[:, 4 * g:4 * (g + 1), :].rearrange("p h w -> p (h w)"), qwT[:],
                                         start=(i == 0), stop=(i == 1), skip_group_check=True)
                    last.then_inc(front_full, 1)

                def scores(b, h):
                    if h == 0:
                        pe.wait_ge(k_ready, b + 1)
                    if h % 8 == 0:
                        pe.wait_ge(q_in[h // 8], (b + 1) * Q_IN)
                    wait(pe, probs_full, b * ROWS + h - 1)
                    for t in range(CT):
                        last = pe.matmul(s_bank[h % 2][:, t, :], q_stack[:, h, t * P:(t + 1) * P], k_stack[:],
                                         start=(t == 0), stop=(t == CT - 1), skip_group_check=True)
                    last.then_inc(s_full, 1)

                def transposes(b, h):
                    pe.wait_ge(probs_full, b * ROWS + h + 1)
                    wait(pe, (evac_even, evac_odd)[h % 2], b * PAIRS + h // 2)
                    for lt in range(LT):
                        for t in range(CT):
                            last = pe.transpose(t_bank[h % 2][:, lt, t * P:(t + 1) * P],
                                                probs[:, h % 2, t, lt * P:(lt + 1) * P], ident[:])
                    last.then_inc(t_full, 1)

                def values(b, p):
                    if p == 0:
                        pe.wait_ge(v_ready, b + 1)
                    pe.wait_ge(evac_even, b * PAIRS + p + 1)
                    pe.wait_ge(evac_odd, b * PAIRS + p + 1)
                    wait(pe, ctxT_full, b * PAIRS + p)
                    for lt in range(LT):
                        last = pe.matmul(o_bank[0:KD + 1, :], v_ones[:, lt, :],
                                         probsT[:, p % 2, lt, :, :], start=(lt == 0), stop=(lt == LT - 1))
                    last.then_inc(o_full, 1)

                def turn_context(b, p):
                    pe.wait_ge(ctxT_full, b * PAIRS + p + 1)
                    wait(pe, ctx_done, b * PAIRS + p)
                    for n in range(4):
                        last = pe.transpose(c_bank[:, n, :], ctxT[:, p % 2, n * P:(n + 1) * P], ident[0:TURN, 0:TURN])
                    last.then_inc(c_full, 1)

                def project(b, k):
                    pe.wait_ge(ctx_done, b * PAIRS + (k + 1) * PAIRS // 2)
                    if k == 0 and has(b + 1):
                        pe.wait_ge(q_low_done, Q_CHUNKS * (b + 1) + Q_CHUNKS - 1)
                    elif k == 1 and has(b + 2):
                        pe.wait_ge(gvar_ready, b + 3)
                    elif k == 1 and has(b + 1):
                        pe.wait_ge(q_low_done, Q_CHUNKS * NB)
                    else:
                        pe.wait_ge(out_done, OUT_USES * b + k)
                    for t in range(CT):
                        last = pe.matmul(front[:], owT[:, t, :], context[:, t, 16 * k:16 * (k + 1), :],
                                         start=(t == 0), stop=(t == CT - 1))
                    last.then_inc(front_full, 1)

                def front_part(b, i):
                    if i == 1:
                        wait(pe, q_low_done, Q_CHUNKS * b)
                        group_sum(b, 0, chan_stats_ready, mv[:, 0:1])
                    if i == 2:
                        group_sum(b, 1, spread_ready, spread[:])
                    if i == 5:
                        keys_values(b)
                    if i in Q_STEPS:
                        queries(b, Q_STEPS.index(i))

                for i in range(PAIRS):
                    front_part(0, i)

                def period(b):
                    for i in range(PAIRS if has(b) else 4):
                        if has(b):
                            scores(b, 2 * i)
                            scores(b, 2 * i + 1)
                        turned, p = pair(b, i - 1)
                        if has(turned):
                            transposes(turned, 2 * p)
                            transposes(turned, 2 * p + 1)
                        if has(pair(b, i - 2)[0]):
                            values(*pair(b, i - 2))
                        if has(pair(b, i - 3)[0]):
                            turn_context(*pair(b, i - 3))
                        if has(b + 1):
                            front_part(b + 1, i)
                        if i == 3 and has(b - 1):
                            project(b - 1, 1)
                        if i == 13:
                            project(b, 0)

                over_images(pe, NB, period)


ATTN_EPS = 1e-9
LN_EPS = 1e-5
TT = HW // P
EXPERTS = 8
TOP = 2
HIDDEN = 341
GROUPS = TOP * EXPERTS
CHUNKS = 3
CHUNK = 114
ROW = 132
GATE, TOKEN = P, P + TOP
BIG = 3.0e38
DUMMIES = 8
F_BF = mybir.dt.bfloat16
I32 = mybir.dt.int32

SHARED = (("x0", 1, 0, 0), ("x1", 1, 0, 1), ("c", -2, 2, 0), ("e0", 1, 3, 1), ("e1", 1, 4, 0), ("g0", 1, 4, 1),
          ("g1", 1, 5, 0), ("r0", -1, 5, 1), ("r1", -1, 6, 0), ("l", -1, 6, 1), ("v0", 1, 7, 0), ("v1", 1, 7, 1))
KINDS = [use[0] for use in SHARED]
STATS_AT, NORM_AT, TARGETS_AT, ROUTE_STATS_AT, ROUTE_NORM_AT, CHOOSE_AT = 1, 2, 3, 3, 4, 7
SCATTERS_AT = {3: (0, 1), 4: (2, 3, 4), 5: (5, 6, 7), 6: (8, 9, 10, 11), 7: (12, 13, 14, 15)}
SUMS = 4


def over_image_pairs(eng, n, period):
    assert n % 2 == 0
    for b in (-1, 0, 1):
        period(b, b % 2)
    if n > 4:
        with eng.Fori(1, n // 2 - 1) as pair:
            period(2 * pair, 0)
            period(2 * pair + 1, 1)
    for b in range(max(n - 2, 2), n + 2):
        period(b, b % 2)


def attention_and_routing(nc, X, ident, table, routed, dram, load_experts):
    NB = X.shape[1]
    NTOK = NB * HW
    REGION = NTOK + P
    TILES = NTOK // P + DUMMIES
    PER_IMAGE = 16 * TT * TOP
    XT = X[:].rearrange("p b (t c) -> p b t c", c=P)
    with ExitStack() as ctx:
        def sb(name, shape, dt=F32):
            return ctx.enter_context(nc.sbuf_tensor("a_" + name, shape, dt))

        def ps(name, shape):
            return ctx.enter_context(nc.psum_tensor("a_" + name, shape, F32))

        def sem(name):
            return ctx.enter_context(nc.semaphore("a_" + name))

        minus_half = sb("minus_half", [P, TT])
        tril = sb("tril", [P, P])
        wq = sb("wq", [P, P])
        wk = sb("wk", [P, P])
        wvT = sb("wvT", [P, P])
        wqk = sb("wqk", [P, P])
        ln_st = sb("ln_st", [P, TT, 6])
        ln_mv = sb("ln_mv", [P, TT, 2])
        ln_ve = sb("ln_ve", [P, TT])
        ln_rs = sb("ln_rs", [P, TT])
        staged = sb("staged", [P, TT, P])
        e_tok = sb("e_tok", [P, TT, P])
        eT = sb("eT", [P, 2, HW])
        gT = sb("gT", [P, 2, HW])
        val = sb("val", [P, 2, TT, P])
        neg_max = sb("row_neg_max", [P, 2])
        probs = sb("causal_probs", [P, 2, HW])
        probsT = sb("causal_probsT", [P, 2, TT, P])
        row_sum = sb("row_sum", [P, SUMS])
        row_eps = sb("row_eps", [P, SUMS])
        row_inv = sb("row_inv", [P, SUMS])

        nothing = sb("nothing", [P, 1], I32)
        waited = sb("waited", [P, 1], I32)
        rwT = sb("rwT", [P, EXPERTS])
        ones = sb("ones", [P, P], F_BF)
        before = sb("before", [P, P], F_BF)
        expert_i = sb("expert_i", [P, TT, EXPERTS], I32)
        expert_no = sb("expert_no", [P, TT, EXPERTS])
        group_i = sb("group_i", [P, GROUPS], I32)
        group_row = sb("group_row", [P, GROUPS])
        next_row = sb("next_row", [P, 2, GROUPS])
        token_i = sb("token_i", [P, NB, TT], I32)
        pad = sb("pad", [P, ROW])
        lane_i = sb("lane_i", [P, 1], I32)
        pad_idx = sb("pad_idx", [P, GROUPS], I32)
        rt_st = sb("rt_st", [P, TT, 6])
        rt_mv = sb("rt_mv", [P, TT, 2])
        rt_ve = sb("rt_ve", [P, TT])
        rt_rs = sb("rt_rs", [P, TT])
        rows = sb("rows", [P, 2, TT, ROW])
        rT = sb("rT", [P, HW])
        logits = sb("logits", [P, TT, EXPERTS])
        rest = sb("rest", [P, TT, EXPERTS])
        top = sb("top", [P, TOP, TT])
        below = sb("below", [P, TT, EXPERTS])
        numbered = sb("numbered", [P, TT, EXPERTS])
        chosen = sb("chosen", [P, TOP, TT])
        pick = sb("pick", [P, TOP, TT, EXPERTS])
        pick_bf = sb("pick_bf", [P, TT, TOP, EXPERTS], F_BF)
        ex_in = sb("ex_in", [P, TT, EXPERTS + 1])
        ex = sb("ex", [P, TT, EXPERTS + 1])
        ex_sum = sb("ex_sum", [P, TT])
        den0 = sb("den0", [P, TT])
        den = sb("den", [P, TT])
        gate0 = sb("gate0", [P, TT])
        counts = sb("counts", [P, TT + 1, GROUPS])
        place = sb("place", [P, TT, GROUPS])
        placed = sb("placed", [P, TT, GROUPS])
        target = sb("target", [P, TT, TOP])
        target_idx = sb("target_idx", [P, 2, TT, TOP], I32)
        amount = sb("amount", [P, GROUPS])
        amount_i = sb("amount_i", [P, GROUPS], I32)
        ntiles_i = sb("ntiles_i", [P, GROUPS], I32)
        ntiles = sb("ntiles", [P, GROUPS])
        ends = sb("ends", [P, GROUPS])
        one_row = sb("one_row", [P, GROUPS])
        offset = sb("offset", [P, TOP, EXPERTS + 1])
        step_up = sb("step_up", [P, TOP, EXPERTS])
        tile_i = sb("tile_i", [1, TOP, TILES, EXPERTS], I32)
        tile_no = sb("tile_no", [1, TOP, TILES, EXPERTS])
        passed = sb("passed", [1, TOP, TILES, EXPERTS])
        jumps = tile_no
        tile_sum = sb("tile_sum", [1, TOP, TILES])
        tile_at = sb("tile_at", [1, TOP, TILES])
        tile_row = sb("tile_row", [1, TOP, TILES])
        tile_expert = sb("tile_expert", [1, TOP, TILES])

        s_bank = [ps(f"score_bank{i}", [P, HW]) for i in range(2)]
        t_bank = ps("turn_bank", [P, TT, P])
        o_bank = ps("sum_bank", [P, P])
        shared = ps("shared_bank", [P, 512])

        weights_in = sem("weights_in")
        staged_in = sem("staged_in")
        consts = sem("consts")
        iotas = sem("iotas")
        cleared = sem("cleared")
        carried = sem("carried")
        casts = sem("casts")
        wqk_mm = sem("wqk_mm")
        wqk_ready = sem("wqk_ready")
        shared_full = sem("shared_full")
        shared_free = sem("shared_free")
        mv_ready = sem("ln_mv_ready")
        ve_ready = sem("ln_ve_ready")
        rs_ready = sem("ln_rs_ready")
        e_ready = sem("e_ready")
        s_full = sem("tile_scored")
        max_ready = sem("row_max_ready")
        exp_done = sem("exp_done")
        diag_done = sem("diagonal_masked")
        masked = sem("tile_masked")
        t_full = sem("tile_turned")
        turned_out = sem("tile_turned_out")
        o_full = sem("tile_summed")
        eps_added = sem("eps_added")
        inv_ready = sem("row_inv_ready")
        added = sem("tile_added")
        rt_ve_ready = sem("rt_ve_ready")
        rt_rs_ready = sem("rt_rs_ready")
        rows_ready = sem("rows_ready")
        ex_in_ready = sem("ex_in_ready")
        ex_ready = sem("ex_ready")
        picks_ready = sem("picks_ready")
        gates_ready = sem("gates_ready")
        targets_ready = sem("targets_ready")
        scattered = [sem(f"scattered{i}") for i in range(2)]
        pad_idx_ready = sem("pad_idx_ready")
        pads = sem("pads")
        table_step = sem("table_step")
        chain = {n: sem("chain_" + n) for n in (
            "mv top0 below0 numbered0 chosen0 pick0 rest top1 below1 numbered1 chosen1 pick1 "
            "ex_sum den0 den gate0 place placed target").split()}

        def has(b):
            return not isinstance(b, int) or 0 <= b < NB

        def uses(b):
            return [kind for kind, back, _, _ in SHARED if has(b + back)]

        def uses_before(b):
            if isinstance(b, int):
                return sum(len(uses(q)) for q in range(-1, b))
            return uses_before(2) + len(SHARED) * (b - 2)

        def use_no(b, kind):
            return uses_before(b) + (uses(b).index(kind) if isinstance(b, int) else KINDS.index(kind))

        def tile(b, slot, i):
            return (b, slot, i) if i >= 0 else (b - 1, 1 - slot, i + TT)

        with nc.Block() as block:

            @block.sync
            def _(sp):
                for dst, src in ((wq, "wq"), (wk, "wk"), (wvT, "wvT"), (rwT, "rwT")):
                    sp.dma_start(dst[:], dram[src]).then_inc(weights_in, 16)

                def stage(b):
                    sp.dma_start(staged[:], XT[:, b, :, :]).then_inc(staged_in, 16)

                stage(0)
                load_experts(sp)
                with sp.Fori(1, NB) as b:
                    sp.wait_ge(e_ready, b)
                    stage(b)
                sp.wait_ge(pad_idx_ready, 1)
                for g in range(GROUPS):
                    row = sp.value_load(pad_idx[0:1, g:g + 1], min_val=0, max_val=GROUPS * REGION - P)
                    sp.dma_start(routed[bass.ds(row, P), :], pad[:]).then_inc(pads, 16)
                sp.wait_ge(pads, 16 * GROUPS)

            @block.gpsimd
            def _(pool):
                pool.memset(nothing[:], 0).then_inc(carried, 1)
                pool.memset(minus_half[:], -0.5).then_inc(consts, 1)
                pool.memset(tril[:], 1.0).then_inc(consts, 1)
                pool.memset(ones[:], 1.0).then_inc(consts, 1)
                pool.memset(before[:], 1.0).then_inc(consts, 1)
                pool.wait_ge(consts, 4)
                pool.affine_select(out=tril[:], in_=tril[:], compare_op=ALU.is_ge, fill=0.0, base=0,
                                   pattern=[[-1, P]], channel_multiplier=1).then_inc(consts, 1)
                pool.affine_select(out=before[:], in_=before[:], compare_op=ALU.is_gt, fill=0.0, base=0,
                                   pattern=[[1, P]], channel_multiplier=-1).then_inc(consts, 1)
                pool.wait_ge(consts, 6)
                pool.iota(expert_i[:], [[0, TT], [1, EXPERTS]], base=0, channel_multiplier=0)
                pool.iota(group_i[:], [[REGION // P, GROUPS]], base=0, channel_multiplier=0)
                pool.iota(token_i[:], [[HW, NB], [P, TT]], base=0, channel_multiplier=1)
                pool.iota(lane_i[:], [[0, 1]], base=0, channel_multiplier=1)
                pool.iota(tile_i[:], [[0, TOP], [1, TILES], [0, EXPERTS]], base=0,
                          channel_multiplier=0).then_inc(iotas, 1)
                pool.wait_ge(casts, 1)
                for d in range(DUMMIES):
                    at = GROUPS * REGION + d * P
                    pool.dma_start(routed[at:at + P, :], pad[:]).then_inc(scattered[d % 2], 16)

                def period(b, slot):
                    for i in range(TT):
                        if has(b):
                            pool.wait_ge(exp_done, b * TT + i + 1)
                            block_ = probs[:, i % 2, i * P:(i + 1) * P]
                            pool.tensor_tensor(block_, block_, tril[:], ALU.mult).then_inc(diag_done, 1)
                        if i == STATS_AT and has(b + 1):
                            pool.wait_ge(ve_ready, b + 2)
                            pool.tensor_tensor(ln_rs[:], ln_ve[:], minus_half[:], ALU.pow).then_inc(rs_ready, 1)
                        if i in SCATTERS_AT and has(b - 2):
                            if i == min(SCATTERS_AT):
                                pool.wait_ge(gates_ready, b - 1)
                                pool.wait_ge(targets_ready, b - 1)
                                pool.wait_ge(carried, b - 1)
                                pool.tensor_tensor(waited[:], nothing[:], nothing[:], ALU.add).then_inc(carried, 1)
                            for n in SCATTERS_AT[i]:
                                t, k = n // TOP, n % TOP
                                pool.indirect_dma_start(
                                    out=routed,
                                    out_offset=bass.IndirectOffsetOnAxis(ap=target_idx[:, slot, t, k:k + 1], axis=0),
                                    in_=rows[:, slot, t, :], in_offset=None).then_inc(scattered[slot], 16)
                        if i == ROUTE_STATS_AT and has(b - 1):
                            pool.wait_ge(rt_ve_ready, b)
                            pool.tensor_tensor(rt_rs[:], rt_ve[:], minus_half[:], ALU.pow).then_inc(rt_rs_ready, 1)

                over_image_pairs(pool, NB, period)
                for i in range(2):
                    pool.wait_ge(scattered[i], 8 * DUMMIES + PER_IMAGE // 2 * NB)

            @block.vector
            def _(dve):
                dve.memset(rows[:], 0.0)
                dve.memset(pad[:], 0.0)
                dve.memset(one_row[:], 1.0).then_inc(cleared, 1)
                dve.wait_ge(cleared, 1)
                dve.wait_ge(iotas, 1)
                dve.tensor_copy(expert_no[:], expert_i[:])
                dve.tensor_copy(tile_no[:], tile_i[:])
                dve.tensor_scalar(group_row[:], group_i[:], float(P), None, ALU.mult)
                dve.tensor_scalar(next_row[:, 0, :], group_i[:], float(P), None, ALU.mult)
                dve.tensor_scalar(tile_at[:], tile_i[:, :, :, 0], float(P), None, ALU.mult)
                dve.tensor_scalar(pad[:, TOKEN:TOKEN + 1].bitcast(I32), lane_i[:], float(NTOK), None,
                                  ALU.add).then_inc(casts, 1)
                dve.wait_ge(casts, 1)
                dve.wait_ge(wqk_mm, 1)
                dve.tensor_scalar(wqk[:], shared[:, 0:P], float(P) ** -0.5, None, ALU.mult).then_inc(wqk_ready, 1)

                def then(name, r, ins):
                    ins.then_inc(chain[name], 1)
                    dve.wait_ge(chain[name], r + 1)

                def token_stats(b):
                    dve.wait_ge(shared_free, use_no(b - 1, "x1") + 1)
                    for t in range(TT):
                        dve.bn_stats(ln_st[:, t, :], XT[:, b, t, :])
                    dve.drain()
                    for t in range(TT):
                        last = dve.bn_aggr(ln_mv[:, t, :], ln_st[:, t, :])
                    last.then_inc(mv_ready, 1)
                    dve.wait_ge(mv_ready, b + 1)
                    dve.tensor_scalar(ln_ve[:], ln_mv[:, :, 1], LN_EPS, None, ALU.add).then_inc(ve_ready, 1)

                def token_norm(b):
                    dve.wait_ge(rs_ready, b + 1)
                    if not (isinstance(b, int) and b == 0):
                        dve.wait_ge(shared_full, use_no(b - 2, "e1") + 1)
                    for t in range(TT):
                        last = dve.tensor_scalar(e_tok[:, t, :], XT[:, b, t, :], ln_mv[:, t, 0:1],
                                                 ln_rs[:, t:t + 1], ALU.subtract, ALU.mult)
                    last.then_inc(e_ready, 1)

                def tile_max(b, i):
                    dve.wait_ge(s_full, b * TT + i + 1)
                    wait(dve, exp_done, b * TT + i - 1)
                    dve.tensor_reduce(neg_max[:, i % 2:i % 2 + 1], s_bank[i % 2][:], AX_X, ALU.max,
                                      negate=True).then_inc(max_ready, 1)

                def mask(b, slot, i):
                    n = (i + 1) * P
                    one = slice(i % SUMS, i % SUMS + 1)
                    dve.wait_ge(diag_done, b * TT + i + 1)
                    dve.scalar_tensor_tensor(out=probs[:, i % 2, 0:n], in0=s_bank[i % 2][:, 0:n], scalar=0.0,
                                             in1=probs[:, i % 2, 0:n], op0=ALU.not_equal, op1=ALU.mult,
                                             accum_out=row_sum[:, one]).then_inc(masked, 1)
                    dve.wait_ge(masked, b * TT + i + 1)
                    dve.tensor_scalar(row_eps[:, one], row_sum[:, one], ATTN_EPS, None, ALU.add).then_inc(eps_added, 1)
                    dve.wait_ge(eps_added, b * TT + i + 1)
                    dve.reciprocal(row_inv[:, one], row_eps[:, one]).then_inc(inv_ready, 1)

                def add(b, slot, i):
                    one = slice(i % SUMS, i % SUMS + 1)
                    dve.wait_ge(inv_ready, b * TT + i + 1)
                    dve.wait_ge(o_full, b * TT + i + 1)
                    dve.scalar_tensor_tensor(out=XT[:, b, i, :], in0=o_bank[:], scalar=row_inv[:, one],
                                             in1=XT[:, b, i, :], op0=ALU.mult, op1=ALU.add).then_inc(added, 1)

                def route_stats(r):
                    dve.drain()
                    for t in range(TT):
                        dve.bn_stats(rt_st[:, t, :], XT[:, r, t, :])
                    dve.drain()
                    for t in range(TT):
                        last = dve.bn_aggr(rt_mv[:, t, :], rt_st[:, t, :])
                    then("mv", r, last)
                    dve.tensor_scalar(rt_ve[:], rt_mv[:, :, 1], LN_EPS, None, ALU.add).then_inc(rt_ve_ready, 1)

                def route_norm(r, slot):
                    dve.wait_ge(rt_rs_ready, r + 1)
                    if not (isinstance(r, int) and r < 2):
                        dve.wait_ge(scattered[slot], 8 * DUMMIES + PER_IMAGE // 2 * (r - slot))
                    for t in range(TT):
                        dve.tensor_scalar(rows[:, slot, t, 0:P], XT[:, r, t, :], rt_mv[:, t, 0:1],
                                          rt_rs[:, t:t + 1], ALU.subtract, ALU.mult)
                    dve.tensor_copy(rows[:, slot, :, TOKEN].bitcast(I32), token_i[:, r, :]).then_inc(rows_ready, 1)

                def per_tile(a):
                    return a.unsqueeze(2).to_broadcast([P, TT, EXPERTS])

                def choose_one(r, k, source):
                    then(f"top{k}", r, dve.tensor_reduce(top[:, k, :], source[:], AX_X, ALU.max))
                    then(f"below{k}", r, dve.tensor_tensor(below[:], source[:], per_tile(top[:, k, :]), ALU.is_lt))
                    then(f"numbered{k}", r, dve.scalar_tensor_tensor(
                        out=numbered[:], in0=below[:], scalar=float(EXPERTS), in1=expert_no[:],
                        op0=ALU.mult, op1=ALU.add))
                    then(f"chosen{k}", r, dve.tensor_reduce(chosen[:, k, :], numbered[:], AX_X, ALU.min))
                    then(f"pick{k}", r, dve.tensor_tensor(pick[:, k, :, :], expert_no[:], per_tile(chosen[:, k, :]),
                                                          ALU.is_equal))

                def choose(r):
                    dve.wait_ge(shared_free, use_no(r + 1, "l") + 1)
                    choose_one(r, 0, logits)
                    then("rest", r, dve.scalar_tensor_tensor(
                        out=rest[:], in0=pick[:, 0, :, :], scalar=-BIG, in1=logits[:], op0=ALU.mult, op1=ALU.add))
                    choose_one(r, 1, rest)
                    dve.tensor_copy(pick_bf[:], pick[:].rearrange("p k t e -> p t k e")).then_inc(picks_ready, 1)
                    dve.tensor_tensor(ex_in[:, :, 0:EXPERTS], logits[:], per_tile(top[:, 0, :]), ALU.subtract)
                    dve.tensor_tensor(ex_in[:, :, EXPERTS], top[:, 1, :], top[:, 0, :], ALU.subtract
                                      ).then_inc(ex_in_ready, 1)

                def gates(r, slot):
                    dve.wait_ge(ex_ready, r + 1)
                    then("ex_sum", r, dve.tensor_reduce(ex_sum[:], ex[:, :, 0:EXPERTS], AX_X, ALU.add))
                    then("den0", r, dve.scalar_tensor_tensor(out=den0[:], in0=ex_sum[:], scalar=1e-9,
                                                             in1=ex[:, :, EXPERTS], op0=ALU.mult, op1=ALU.add))
                    then("den", r, dve.tensor_scalar(den[:], den0[:], 1.0, None, ALU.add))
                    then("gate0", r, dve.reciprocal(gate0[:], den[:]))
                    dve.tensor_copy(rows[:, slot, :, GATE], gate0[:])
                    dve.tensor_tensor(rows[:, slot, :, GATE + 1], gate0[:], ex[:, :, EXPERTS], ALU.mult
                                      ).then_inc(gates_ready, 1)

                def targets(r, parity):
                    dve.wait_ge(shared_free, use_no(r + 2, "c") + 1)
                    carry = next_row[:, parity, :]
                    by_choice = lambda a: a[:].rearrange("p t (k e) -> p t k e", k=TOP)
                    dve.tensor_tensor(next_row[:, 1 - parity, :], carry, counts[:, TT, :], ALU.add)
                    then("place", r, dve.tensor_tensor(place[:], counts[:, 0:TT, :],
                                                       carry.unsqueeze(1).to_broadcast([P, TT, GROUPS]), ALU.add))
                    then("placed", r, dve.tensor_tensor(by_choice(placed), by_choice(place), pick_bf[:], ALU.mult))
                    then("target", r, dve.tensor_reduce(target[:], by_choice(placed), AX_X, ALU.add))
                    dve.tensor_copy(target_idx[:, parity], target[:]).then_inc(targets_ready, 1)

                def period(b, slot):
                    for i in range(TT):
                        before_ = tile(b, slot, i - 1)
                        if has(before_[0]):
                            mask(*before_)
                        if has(b):
                            tile_max(b, i)
                        summed = tile(b, slot, i - 3)
                        if has(summed[0]):
                            add(*summed)
                        if i == 0 and has(b - 2):
                            gates(b - 2, slot)
                        if i == STATS_AT and has(b + 1):
                            token_stats(b + 1)
                        if i == NORM_AT and has(b + 1):
                            token_norm(b + 1)
                        if i == TARGETS_AT and has(b - 2):
                            targets(b - 2, slot)
                        if i == ROUTE_STATS_AT and has(b - 1):
                            route_stats(b - 1)
                        if i == ROUTE_NORM_AT and has(b - 1):
                            route_norm(b - 1, 1 - slot)
                        if i == CHOOSE_AT and has(b - 1):
                            choose(b - 1)

                over_image_pairs(dve, NB, period)

                n = [0]

                def step(ins):
                    ins.then_inc(table_step, 1)
                    n[0] += 1
                    dve.wait_ge(table_step, n[0])

                final = next_row[:, NB % 2, :]
                step(dve.tensor_tensor(amount[:], final, group_row[:], ALU.subtract))
                dve.tensor_copy(pad_idx[:], final).then_inc(pad_idx_ready, 1)
                step(dve.tensor_scalar(amount_i[:], amount[:], float(P - 1), None, ALU.add))
                step(dve.tensor_scalar(ntiles_i[:], amount_i[:], P.bit_length() - 1, None, ALU.logical_shift_right))
                step(dve.tensor_copy(ntiles[:], ntiles_i[:]))
                for k in range(TOP):
                    g = slice(k * EXPERTS, (k + 1) * EXPERTS)
                    step(dve.tensor_tensor_scan(ends[:, g], one_row[:, g], ntiles[:, g], 0.0, ALU.mult, ALU.add))
                step(dve.tensor_tensor(amount[:], ends[:], ntiles[:], ALU.subtract))
                by_choice = lambda a: a[:].rearrange("p (k e) -> p k e", k=TOP)
                step(dve.scalar_tensor_tensor(out=offset[:, :, 0:EXPERTS], in0=by_choice(amount), scalar=-float(P),
                                              in1=by_choice(group_row), op0=ALU.mult, op1=ALU.add))
                step(dve.tensor_scalar(offset[:, :, EXPERTS], by_choice(ends)[:, :, EXPERTS - 1], -float(P),
                                       float(GROUPS * REGION), ALU.mult, ALU.add))
                step(dve.tensor_tensor(step_up[:], offset[:, :, 1:], offset[:, :, 0:EXPERTS], ALU.subtract))
                for k in range(TOP):
                    every = lambda a: a.unsqueeze(1).to_broadcast([1, TILES, EXPERTS])
                    step(dve.tensor_tensor(passed[:, k], tile_no[:, k], every(by_choice(ends)[0:1, k, :]), ALU.is_ge))
                    step(dve.tensor_tensor(jumps[:, k], passed[:, k], every(step_up[0:1, k, :]), ALU.mult))
                step(dve.tensor_reduce(tile_sum[:], jumps[:], AX_X, ALU.add))
                step(dve.tensor_tensor(tile_row[:], tile_at[:], tile_sum[:], ALU.add))
                step(dve.tensor_reduce(tile_expert[:], passed[:], AX_X, ALU.add))
                for k in range(TOP):
                    of_choice = slice(k * TILES, (k + 1) * TILES)
                    step(dve.tensor_scalar(table[:, 0, of_choice], tile_row[:, k, :], offset[0:1, k, 0:1], None, ALU.add))
                    step(dve.tensor_scalar(table[:, 1, of_choice], tile_expert[:, k, :], float(EXPERTS - 1), None, ALU.min))

            @block.scalar
            def _(act):
                def shared_out(b, slot, kind, back):
                    act.wait_ge(shared_full, use_no(b, kind) + 1)
                    h = int(kind[1]) if len(kind) > 1 else 0
                    half = slice(512 * h, 512 * (h + 1))
                    tiles = slice(TT // 2 * h, TT // 2 * (h + 1))
                    by_tile = shared[:].rearrange("p (t c) -> p t c", c=P)
                    dst, src = {
                        "x": lambda: (XT[:, b + back, tiles, :], by_tile),
                        "e": lambda: (eT[:, 1 - slot, half], shared[:]),
                        "g": lambda: (gT[:, 1 - slot, half], shared[:]),
                        "v": lambda: (val[:, 1 - slot, tiles, :], by_tile),
                        "r": lambda: (rT[:, half], shared[:]),
                        "l": lambda: (logits[:], shared[:, 0:TT * EXPERTS].rearrange("p (t e) -> p t e", e=EXPERTS)),
                        "c": lambda: (counts[:], shared[:, 0:(TT + 1) * GROUPS].rearrange("p (t g) -> p t g", g=GROUPS)),
                    }[kind[0]]()
                    act.activation(dst, src, ACT.Copy).then_inc(shared_free, 1)

                def exps(b, i):
                    act.wait_ge(max_ready, b * TT + i + 1)
                    wait(act, t_full, b * TT + i - 1)
                    n = (i + 1) * P
                    act.activation(probs[:, i % 2, 0:n], s_bank[i % 2][:, 0:n], ACT.Exp,
                                   bias=neg_max[:, i % 2:i % 2 + 1]).then_inc(exp_done, 1)

                def turned(b, slot, i):
                    act.wait_ge(t_full, b * TT + i + 1)
                    wait(act, o_full, b * TT + i - 1)
                    act.activation(probsT[:, i % 2, 0:i + 1, :], t_bank[:, 0:i + 1, :], ACT.Copy
                                   ).then_inc(turned_out, 1)

                def gate_exps(r):
                    act.wait_ge(ex_in_ready, r + 1)
                    act.activation(ex[:], ex_in[:], ACT.Exp).then_inc(ex_ready, 1)

                def period(b, slot):
                    def outs(i, place_):
                        for kind, back, at, where in SHARED:
                            if (at, where) == (i, place_) and has(b + back):
                                shared_out(b, slot, kind, back)

                    for i in range(TT):
                        if i == 0 and has(b - 2):
                            gate_exps(b - 2)
                        outs(i, 0)
                        turned_ = tile(b, slot, i - 2)
                        if has(turned_[0]):
                            turned(*turned_)
                        if has(b):
                            exps(b, i)
                        outs(i, 1)

                over_image_pairs(act, NB, period)

            @block.tensor
            def _(pe):
                pe.wait_ge(weights_in, 64)
                pe.wait_ge(iotas, 1)
                pe.matmul(shared[:, 0:P], wq[:], wk[:], start=True, stop=True).then_inc(wqk_mm, 1)
                pe.wait_ge(wqk_ready, 1)

                def shared_use(b, slot, kind):
                    what = kind[0]
                    h = int(kind[1]) if len(kind) > 1 else 0
                    wait(pe, shared_free, use_no(b, kind))
                    if kind == "x0":
                        pe.wait_ge(staged_in, 16 * (b + 2))
                    if kind == "e0":
                        pe.wait_ge(e_ready, b + 2)
                    if kind == "r0":
                        pe.wait_ge(rows_ready, b)
                    if what == "c":
                        pe.wait_ge(picks_ready, b - 1)
                        counts_bank = shared[:, 0:(TT + 1) * GROUPS].rearrange("p (t g) -> p t g", g=GROUPS)
                        pe.matmul(shared[:, 0:TT * GROUPS], before[:], pick_bf[:].rearrange("p t k e -> p (t k e)"),
                                  start=True, stop=False, skip_group_check=True)
                        for t in range(TT):
                            last = pe.matmul(counts_bank[:, t + 1:, :], ones[:],
                                             pick_bf[:, t, :, :].rearrange("p k e -> p (k e)").unsqueeze(1)
                                             .to_broadcast([P, TT - t, GROUPS]),
                                             start=False, stop=(t == TT - 1), skip_group_check=True)
                    elif what == "l":
                        for t in range(TT):
                            last = pe.matmul(shared[:, EXPERTS * t:EXPERTS * (t + 1)], rT[:, t * P:(t + 1) * P], rwT[:],
                                             start=(t == 0), stop=(t == TT - 1), skip_group_check=True)
                    elif what == "g":
                        last = pe.matmul(shared[:], wqk[:], eT[:, 1 - slot, 512 * h:512 * (h + 1)],
                                         start=True, stop=True)
                    else:
                        for n in range(TT // 2):
                            t = TT // 2 * h + n
                            out = shared[:, n * P:(n + 1) * P]
                            if what == "x":
                                last = pe.transpose(out, staged[:, t, :], ident[:])
                            elif what == "e":
                                last = pe.transpose(out, e_tok[:, t, :], ident[:])
                            elif what == "r":
                                last = pe.transpose(out, rows[:, 1 - slot, t, 0:P], ident[:])
                            else:
                                last = pe.matmul(out, eT[:, 1 - slot, t * P:(t + 1) * P], wvT[:], start=(n == 0),
                                                 stop=(n == TT // 2 - 1), skip_group_check=True)
                    last.then_inc(shared_full, 1)

                def scores(b, slot, i):
                    if i == 0:
                        pe.wait_ge(shared_free, use_no(b - 1, "g1") + 1)
                    wait(pe, masked, b * TT + i - 1)
                    for h in range(2):
                        last = pe.matmul(s_bank[i % 2][:, 512 * h:512 * (h + 1)], gT[:, slot, i * P:(i + 1) * P],
                                         eT[:, slot, 512 * h:512 * (h + 1)], start=True, stop=True)
                    last.then_inc(s_full, 1)

                def turn(b, slot, i):
                    pe.wait_ge(masked, b * TT + i + 1)
                    wait(pe, turned_out, b * TT + i)
                    for t in range(i + 1):
                        last = pe.transpose(t_bank[:, t, :], probs[:, i % 2, t * P:(t + 1) * P], ident[:])
                    last.then_inc(t_full, 1)

                def values(b, slot, i):
                    if i == 0:
                        pe.wait_ge(shared_free, use_no(b - 1, "v1") + 1)
                    pe.wait_ge(turned_out, b * TT + i + 1)
                    wait(pe, added, b * TT + i)
                    for t in range(i + 1):
                        last = pe.matmul(o_bank[:], probsT[:, i % 2, t, :], val[:, slot, t, :],
                                         start=(t == 0), stop=(t == i))
                    last.then_inc(o_full, 1)

                def period(b, slot):
                    def shared_uses(i, place_):
                        for kind, back, at, where in SHARED:
                            if (at, where) == (i, place_) and has(b + back):
                                shared_use(b, slot, kind)

                    for i in range(TT):
                        if has(b):
                            scores(b, slot, i)
                        shared_uses(i, 0)
                        turned_ = tile(b, slot, i - 2)
                        if has(turned_[0]):
                            turn(*turned_)
                        shared_uses(i, 1)
                        summed = tile(b, slot, i - 3)
                        if has(summed[0]):
                            values(*summed)

                over_image_pairs(pe, NB, period)


RING = 8


def expert_tiles(nc, X, table, routed, answers, ident, w1, w3, w2, weights_in):
    NB = X.shape[1]
    ntok = NB * HW
    TILES = ntok // P + DUMMIES
    ALL = TOP * TILES
    XT = X[:].rearrange("p b (t c) -> p b t c", c=P)
    with ExitStack() as ctx:
        def sb(name, shape, dt=F32):
            return ctx.enter_context(nc.sbuf_tensor("f_" + name, shape, dt))

        def ps(name, shape):
            return ctx.enter_context(nc.psum_tensor("f_" + name, shape, F32))

        def sem(name):
            return ctx.enter_context(nc.semaphore("f_" + name))

        part = sb("part", [P, TT, P])
        rows = sb("rows", [P, RING, ROW])
        nothing = sb("nothing", [P, 1], I32)
        waited = sb("waited", [P, 1], I32)
        xT = sb("xT", [P, 2, P])
        silu = sb("silu", [P, 2, HIDDEN])
        hidden = sb("hidden", [P, 2, CHUNKS * CHUNK])
        hiddenT = sb("hiddenT", [CHUNK, 2, CHUNKS, P])
        y = sb("y", [P, RING, P])

        x_bank = ps("x_bank", [P, P])
        h1_bank = [ps(f"h1_bank{i}", [P, 512]) for i in range(2)]
        h3_bank = [ps(f"h3_bank{i}", [P, 512]) for i in range(2)]
        hT_bank = ps("hT_bank", [CHUNK, CHUNKS, P])
        y_bank = ps("y_bank", [P, P])

        part_free = sem("part_free")
        part_in = sem("part_in")
        cleared = sem("cleared")
        carried = sem("carried")
        row_in = [sem(f"row_in{i}") for i in range(RING)]
        x_turned = sem("x_turned")
        x_out = sem("x_out")
        h_full = sem("h_full")
        silu_done = sem("silu_done")
        gated = sem("gated")
        h_turned = sem("h_turned")
        h_out = sem("h_out")
        y_full = sem("y_full")
        y_out = sem("y_out")
        y_sent = [sem(f"y_sent{i}") for i in range(RING)]

        TURNS = TILES // RING
        assert TURNS == NB + 1

        def passing(q, k):
            return k == 1 and not isinstance(q, int)

        def over_tiles(eng, body):
            def turn(q, k):
                for i in range(RING):
                    body(RING * q + i, q, i, k)

            turn(0, 0)
            turn(1, 0)
            with eng.Fori(2, TURNS) as q:
                turn(q, 0)
            with eng.Fori(TURNS, 2 * TURNS - 1) as q:
                turn(q, 1)
            turn(2 * TURNS - 1, 1)

        def first(n):
            return isinstance(n, int) and n == 0

        def last_one(n):
            return isinstance(n, int) and n == ALL - 1

        def entry(n):
            return slice(n, n + 1) if isinstance(n, int) else bass.ds(n, 1)

        with nc.Block() as block:

            @block.sync
            def _(sp):
                def load(n, q, i, k):
                    row = sp.value_load(table[0:1, 0, entry(n)], min_val=0,
                                        max_val=GROUPS * (ntok + P) + (DUMMIES - 1) * P)
                    wait(sp, y_sent[i], 16 * q)
                    sp.dma_start(rows[:, i, :], routed[bass.ds(row, P), :]).then_inc(row_in[i], 16)
                    if i == RING - 1 and passing(q, k):
                        b = q - TURNS
                        sp.wait_ge(part_free, b + 1)
                        sp.dma_start(part[:], answers[0][bass.ds(b * HW, HW), :].rearrange("(t p) c -> p t c", p=P)
                                     ).then_inc(part_in, 16)

                over_tiles(sp, load)

            @block.gpsimd
            def _(pool):
                pool.memset(nothing[:], 0).then_inc(carried, 1)

                def send(n, q, i, k):
                    pool.wait_ge(y_out, n + 1)
                    pool.wait_ge(carried, n + 1)
                    pool.tensor_tensor(waited[:], nothing[:], nothing[:], ALU.add).then_inc(carried, 1)
                    pool.indirect_dma_start(
                        out=answers[k],
                        out_offset=bass.IndirectOffsetOnAxis(ap=rows[:, i, TOKEN:TOKEN + 1].bitcast(I32), axis=0),
                        in_=y[:, i, :], in_offset=None, bounds_check=ntok - 1, oob_is_err=False
                    ).then_inc(y_sent[i], 16)

                over_tiles(pool, send)
                for i in range(RING):
                    pool.wait_ge(y_sent[i], 16 * (ALL // RING))

            @block.scalar
            def _(act):
                def x_evacuate(n, slot):
                    act.wait_ge(x_turned, n + 1)
                    wait(act, h_full, n - 1)
                    act.activation(xT[:, slot, :], x_bank[:], ACT.Copy).then_inc(x_out, 1)

                def h_evacuate(n, slot):
                    act.wait_ge(h_turned, n + 1)
                    wait(act, y_full, n - 1)
                    act.activation(hiddenT[:, slot, :, :], hT_bank[:], ACT.Copy).then_inc(h_out, 1)

                def body(n, q, i, k):
                    if first(n):
                        x_evacuate(0, 0)
                    if not last_one(n):
                        x_evacuate(n + 1, (i + 1) % 2)
                    act.wait_ge(h_full, n + 1)
                    wait(act, gated, n - 1)
                    act.activation(silu[:, i % 2, :], h1_bank[i % 2][:, 0:HIDDEN], ACT.Silu).then_inc(silu_done, 1)
                    if not first(n):
                        h_evacuate(n - 1, (i + 1) % 2)

                over_tiles(act, body)
                h_evacuate(ALL - 1, 1)

            @block.vector
            def _(dve):
                dve.memset(hidden[:], 0.0).then_inc(cleared, 1)
                dve.memset(part[:, 0, 0:1], 0.0).then_inc(part_free, 1)
                dve.wait_ge(cleared, 1)

                def y_evacuate(n, q, i):
                    dve.wait_ge(y_full, n + 1)
                    wait(dve, y_sent[i], 16 * q)
                    dve.tensor_copy(y[:, i, :], y_bank[:]).then_inc(y_out, 1)

                def body(n, q, i, k):
                    dve.wait_ge(silu_done, n + 1)
                    wait(dve, h_turned, n - 1)
                    dve.scalar_tensor_tensor(out=hidden[:, i % 2, 0:HIDDEN], in0=silu[:, i % 2, :],
                                             scalar=rows[:, i, GATE + k:GATE + k + 1], in1=h3_bank[i % 2][:, 0:HIDDEN],
                                             op0=ALU.mult, op1=ALU.mult).then_inc(gated, 1)
                    if not (isinstance(n, int) and n < 2):
                        y_evacuate(n - 2, q - (i < 2), (i - 2) % RING)

                def body_and_image(n, q, i, k):
                    body(n, q, i, k)
                    if i == RING - 1 and passing(q, k):
                        b = q - TURNS
                        dve.wait_ge(part_in, 16 * (b + 1))
                        image = XT[:, b]
                        dve.tensor_tensor(image, image, part[:], ALU.add).then_inc(part_free, 1)

                over_tiles(dve, body_and_image)
                y_evacuate(ALL - 2, ALL // RING - 1, RING - 2)
                y_evacuate(ALL - 1, ALL // RING - 1, RING - 1)

            @block.tensor
            def _(pe):
                pe.wait_ge(weights_in, 16 * (2 + CHUNKS))

                def turn_rows(n, q, i):
                    pe.wait_ge(row_in[i], 16 * (q + 1))
                    wait(pe, x_out, n)
                    pe.transpose(x_bank[:], rows[:, i, 0:P], ident[:]).then_inc(x_turned, 1)

                experts = {}

                def expert_of(n):
                    return pe.value_load(table[0:1, 1, entry(n)], min_val=0, max_val=EXPERTS - 1)

                def up(n, i, e):
                    pe.wait_ge(x_out, n + 1)
                    wait(pe, gated, n - 1)
                    pe.matmul(h1_bank[i % 2][:, 0:HIDDEN], xT[:, i % 2, :], w1[:, bass.ds(e * HIDDEN, HIDDEN)],
                              start=True, stop=True)
                    pe.matmul(h3_bank[i % 2][:, 0:HIDDEN], xT[:, i % 2, :], w3[:, bass.ds(e * HIDDEN, HIDDEN)],
                              start=True, stop=True).then_inc(h_full, 1)

                def turn_hidden(n, slot):
                    pe.wait_ge(gated, n + 1)
                    wait(pe, h_out, n)
                    for j in range(CHUNKS):
                        last = pe.transpose(hT_bank[:, j, :], hidden[:, slot, j * CHUNK:(j + 1) * CHUNK], ident[:])
                    last.then_inc(h_turned, 1)

                def down(n, slot, e):
                    pe.wait_ge(h_out, n + 1)
                    wait(pe, y_out, n)
                    for j in range(CHUNKS):
                        m = min(CHUNK, HIDDEN - j * CHUNK)
                        last = pe.matmul(y_bank[:], hiddenT[0:m, slot, j, :], w2[0:m, bass.ds(e, 1), j, :],
                                         start=(j == 0), stop=(j == CHUNKS - 1))
                    last.then_inc(y_full, 1)

                def body(n, q, i, k):
                    if first(n):
                        turn_rows(0, 0, 0)
                    experts[i] = expert_of(n)
                    if not last_one(n):
                        turn_rows(n + 1, q + (i == RING - 1), (i + 1) % RING)
                    up(n, i, experts[i])
                    if not first(n):
                        turn_hidden(n - 1, (i + 1) % 2)
                    if not (isinstance(n, int) and n < 2):
                        down(n - 2, i % 2, experts[i - 2] if i >= 2 else expert_of(n - 2))

                over_tiles(pe, body)
                turn_hidden(ALL - 1, 1)
                down(ALL - 2, 0, expert_of(ALL - 2))
                down(ALL - 1, 1, expert_of(ALL - 1))


def add_answers(nc, X, answers, out):
    NB = X.shape[1]
    XT = X[:].rearrange("p b (t c) -> p b t c", c=P)
    SLOTS = 4
    with ExitStack() as ctx:
        parts = ctx.enter_context(nc.sbuf_tensor("parts", [P, SLOTS, TT, P], F32))
        loaded = [ctx.enter_context(nc.semaphore(f"answers_in{i}")) for i in range(SLOTS)]
        summed = ctx.enter_context(nc.semaphore("summed"))
        stored = ctx.enter_context(nc.semaphore("stored"))
        with nc.Block() as block:

            @block.sync
            def _(sp):
                for b in range(NB):
                    wait(sp, summed, b - SLOTS + 1)
                    sp.dma_start(parts[:, b % SLOTS], answers[b * HW:(b + 1) * HW, :]
                                 .rearrange("(t p) c -> p t c", p=P)).then_inc(loaded[b % SLOTS], 16)

            @block.vector
            def _(dve):
                for b in range(NB):
                    dve.wait_ge(loaded[b % SLOTS], 16 * (b // SLOTS + 1))
                    dve.tensor_tensor(XT[:, b], XT[:, b], parts[:, b % SLOTS], ALU.add).then_inc(summed, 1)

            @block.scalar
            def _(act):
                for b in range(NB):
                    act.wait_ge(summed, b + 1)
                    act.dma_start(out[b].rearrange("(t p) c -> p t c", p=P), XT[:, b]).then_inc(stored, 16)
                act.wait_ge(stored, 16 * NB)


def build(nc, dram, out):
    NB = dram["x"].shape[0]
    ntok = NB * HW
    routed = nc.dram_tensor("routed", (GROUPS * (ntok + P) + DUMMIES * P, ROW), F32).ap()
    answers = [nc.dram_tensor(f"answers{k}", (ntok, P), F32).ap() for k in range(TOP)]
    with ExitStack() as ctx:
        X = ctx.enter_context(nc.sbuf_tensor("X", [P, NB, HW], F32))
        ident = ctx.enter_context(nc.sbuf_tensor("ident", [P, P], F32))
        table = ctx.enter_context(nc.sbuf_tensor("table", [1, 2, TOP * (ntok // P + DUMMIES)], I32))
        conv_attention(nc, X, ident, dram)

        w1 = ctx.enter_context(nc.sbuf_tensor("w1", [P, EXPERTS * HIDDEN], F32))
        w3 = ctx.enter_context(nc.sbuf_tensor("w3", [P, EXPERTS * HIDDEN], F32))
        w2 = ctx.enter_context(nc.sbuf_tensor("w2", [CHUNK, EXPERTS, CHUNKS, P], F32))
        experts_in = ctx.enter_context(nc.semaphore("experts_in"))

        def load_experts(sp):
            sp.dma_start(w1[:], dram["w1T"]).then_inc(experts_in, 16)
            sp.dma_start(w3[:], dram["w3T"]).then_inc(experts_in, 16)
            for j in range(CHUNKS):
                n = min(CHUNK, HIDDEN - j * CHUNK)
                sp.dma_start(w2[0:n, :, j, :], dram["w2T"][:, j * CHUNK:j * CHUNK + n, :]
                             .rearrange("e h c -> h e c")).then_inc(experts_in, 16)

        attention_and_routing(nc, X, ident, table, routed, dram, load_experts)
        expert_tiles(nc, X, table, routed, answers, ident, w1, w3, w2, experts_in)
        add_answers(nc, X, answers[1], out)


def kernel(**inputs):
    import numpy as _np
    import concourse.bacc as _bacc
    from concourse import mybir as _mybir
    from concourse.bass_utils import run_bass_kernel_spmd as _run

    x = _np.asarray(inputs["x"])
    B, C, H, W = x.shape
    get = lambda n: _np.asarray(inputs[n])
    laid = {
        "x": x.reshape(B, C, H * W),
        "qWT": get("L0_conv_qW").T, "kWT": get("L0_conv_kW").T, "vWT": get("L0_conv_vW").T,
        "oWT": get("L0_conv_oW").T,
        "kdw": get("L0_conv_kdwW").reshape(C, 9), "vdw": get("L0_conv_vdwW").reshape(C, 9),
        "bn": _np.stack([_np.stack([get(f"L0_conv_{s}dw_{n}") for s in "kv"], 1)
                         for n in ("gamma", "beta", "mean", "var")], 1),
    }
    laid.update(wq=get("L1_attn_WQ"), wk=get("L1_attn_WK"), wvT=get("L1_attn_WV").T)
    hidden_first = lambda n: get(n).transpose(2, 0, 1).reshape(C, -1)
    laid.update(rwT=get("L1_ffn_router_w").T, w1T=hidden_first("L1_ffn_w1"), w3T=hidden_first("L1_ffn_w3"),
                w2T=get("L1_ffn_w2").transpose(0, 2, 1))
    nc = _bacc.Bacc("TRN2", target_bir_lowering=False, num_devices=1)
    arrays, dram = {}, {}
    for name, a in laid.items():
        a = _np.ascontiguousarray(a)
        arrays[f"in_{name}"] = a
        dram[name] = nc.dram_tensor(f"in_{name}", a.shape, _mybir.dt.from_np(a.dtype), kind="ExternalInput").ap()
    out = nc.dram_tensor("out_0", (B, H * W, C), _mybir.dt.float32, kind="ExternalOutput").ap()
    build(nc, dram, out)
    r = _run(nc, [arrays], core_ids=[0])
    return r.results[0]["out_0"].reshape(B, H, W, C).transpose(0, 3, 1, 2)
```
